# Optimizing a Trainium2 kernel written in Bass

```python
import numpy as np
import jax
import jax.numpy as jnp

def _softmax(x, axis=-1):
    return jax.nn.softmax(x, axis=axis)

def _gelu(x):
    return jax.nn.gelu(x, approximate=True)

def _silu(x):
    return jax.nn.silu(x)

def _sigmoid(x):
    return jax.nn.sigmoid(x)

def _layernorm(x, axis=-1, eps=1e-05):
    m = jnp.mean(x, axis=axis, keepdims=True)
    v = jnp.var(x, axis=axis, keepdims=True)
    return (x - m) / jnp.sqrt(v + eps)

def _scatter_add(tgt, idx, src, axis=0):
    return tgt.at[idx].add(src)

def _segment_sum(src, seg, n):
    return jax.ops.segment_sum(src, seg, n)
kernel_name = 'mk_dlrm_tower_d1_rec_r8_778460'

def setup_inputs(seed: int=0):
    np.random.seed(seed)
    _w = jnp.asarray

    def _rec_inputs():
        import jax
        import jax.numpy as jnp
        _tk = jax.random.key(seed)
        dense_ctx = jax.random.normal(jax.random.fold_in(_tk, 190), (1024, 16), jnp.float32)
        ids = jnp.stack([jax.random.randint(jax.random.fold_in(_tk, 200 + f), (1024,), 0, v, jnp.int32) for f, v in enumerate([1250, 12500, 1250, 1000, 1250, 1000, 125000, 125000, 125000, 125000, 1250, 125000, 12500, 12500, 1250, 1250, 1000, 125000, 12500, 125000, 1000, 1250, 12500, 1250, 12500, 1000, 1250, 1000, 1250, 1000, 1250, 1250])], axis=1)
        tbl_0 = 0.05 * jax.random.normal(jax.random.fold_in(_tk, 500 + 0), (1250, 32), jnp.float32)
        tbl_1 = 0.05 * jax.random.normal(jax.random.fold_in(_tk, 500 + 1), (12500, 32), jnp.float32)
        tbl_2 = 0.05 * jax.random.normal(jax.random.fold_in(_tk, 500 + 2), (1250, 32), jnp.float32)
        tbl_3 = 0.05 * jax.random.normal(jax.random.fold_in(_tk, 500 + 3), (1000, 32), jnp.float32)
        tbl_4 = 0.05 * jax.random.normal(jax.random.fold_in(_tk, 500 + 4), (1250, 32), jnp.float32)
        tbl_5 = 0.05 * jax.random.normal(jax.random.fold_in(_tk, 500 + 5), (1000, 32), jnp.float32)
        tbl_6 = 0.05 * jax.random.normal(jax.random.fold_in(_tk, 500 + 6), (125000, 32), jnp.float32)
        tbl_7 = 0.05 * jax.random.normal(jax.random.fold_in(_tk, 500 + 7), (125000, 32), jnp.float32)
        tbl_8 = 0.05 * jax.random.normal(jax.random.fold_in(_tk, 500 + 8), (125000, 32), jnp.float32)
        tbl_9 = 0.05 * jax.random.normal(jax.random.fold_in(_tk, 500 + 9), (125000, 32), jnp.float32)
        tbl_10 = 0.05 * jax.random.normal(jax.random.fold_in(_tk, 500 + 10), (1250, 32), jnp.float32)
        tbl_11 = 0.05 * jax.random.normal(jax.random.fold_in(_tk, 500 + 11), (125000, 32), jnp.float32)
        tbl_12 = 0.05 * jax.random.normal(jax.random.fold_in(_tk, 500 + 12), (12500, 32), jnp.float32)
        tbl_13 = 0.05 * jax.random.normal(jax.random.fold_in(_tk, 500 + 13), (12500, 32), jnp.float32)
        tbl_14 = 0.05 * jax.random.normal(jax.random.fold_in(_tk, 500 + 14), (1250, 32), jnp.float32)
        tbl_15 = 0.05 * jax.random.normal(jax.random.fold_in(_tk, 500 + 15), (1250, 32), jnp.float32)
        tbl_16 = 0.05 * jax.random.normal(jax.random.fold_in(_tk, 500 + 16), (1000, 32), jnp.float32)
        tbl_17 = 0.05 * jax.random.normal(jax.random.fold_in(_tk, 500 + 17), (125000, 32), jnp.float32)
        tbl_18 = 0.05 * jax.random.normal(jax.random.fold_in(_tk, 500 + 18), (12500, 32), jnp.float32)
        tbl_19 = 0.05 * jax.random.normal(jax.random.fold_in(_tk, 500 + 19), (125000, 32), jnp.float32)
        tbl_20 = 0.05 * jax.random.normal(jax.random.fold_in(_tk, 500 + 20), (1000, 32), jnp.float32)
        tbl_21 = 0.05 * jax.random.normal(jax.random.fold_in(_tk, 500 + 21), (1250, 32), jnp.float32)
        tbl_22 = 0.05 * jax.random.normal(jax.random.fold_in(_tk, 500 + 22), (12500, 32), jnp.float32)
        tbl_23 = 0.05 * jax.random.normal(jax.random.fold_in(_tk, 500 + 23), (1250, 32), jnp.float32)
        tbl_24 = 0.05 * jax.random.normal(jax.random.fold_in(_tk, 500 + 24), (12500, 32), jnp.float32)
        tbl_25 = 0.05 * jax.random.normal(jax.random.fold_in(_tk, 500 + 25), (1000, 32), jnp.float32)
        tbl_26 = 0.05 * jax.random.normal(jax.random.fold_in(_tk, 500 + 26), (1250, 32), jnp.float32)
        tbl_27 = 0.05 * jax.random.normal(jax.random.fold_in(_tk, 500 + 27), (1000, 32), jnp.float32)
        tbl_28 = 0.05 * jax.random.normal(jax.random.fold_in(_tk, 500 + 28), (1250, 32), jnp.float32)
        tbl_29 = 0.05 * jax.random.normal(jax.random.fold_in(_tk, 500 + 29), (1000, 32), jnp.float32)
        tbl_30 = 0.05 * jax.random.normal(jax.random.fold_in(_tk, 500 + 30), (1250, 32), jnp.float32)
        tbl_31 = 0.05 * jax.random.normal(jax.random.fold_in(_tk, 500 + 31), (1250, 32), jnp.float32)
        _rk = jax.random.fold_in(_tk, 7)
        W_top1 = 0.0606339 * jax.random.normal(jax.random.fold_in(_tk, 801), (272, 512), jnp.float32)
        W_top2 = 0.0441942 * jax.random.normal(jax.random.fold_in(_tk, 802), (512, 256), jnp.float32)
        W_top3 = 0.0625 * jax.random.normal(jax.random.fold_in(_tk, 803), (256, 1), jnp.float32)
        b_top1 = jnp.zeros((512,), jnp.float32)
        b_top2 = jnp.zeros((256,), jnp.float32)
        return (dense_ctx, ids, tbl_0, tbl_1, tbl_2, tbl_3, tbl_4, tbl_5, tbl_6, tbl_7, tbl_8, tbl_9, tbl_10, tbl_11, tbl_12, tbl_13, tbl_14, tbl_15, tbl_16, tbl_17, tbl_18, tbl_19, tbl_20, tbl_21, tbl_22, tbl_23, tbl_24, tbl_25, tbl_26, tbl_27, tbl_28, tbl_29, tbl_30, tbl_31, W_top1, b_top1, W_top2, b_top2, W_top3)
    dense_ctx, ids, tbl_0, tbl_1, tbl_2, tbl_3, tbl_4, tbl_5, tbl_6, tbl_7, tbl_8, tbl_9, tbl_10, tbl_11, tbl_12, tbl_13, tbl_14, tbl_15, tbl_16, tbl_17, tbl_18, tbl_19, tbl_20, tbl_21, tbl_22, tbl_23, tbl_24, tbl_25, tbl_26, tbl_27, tbl_28, tbl_29, tbl_30, tbl_31, W_top1, b_top1, W_top2, b_top2, W_top3 = _rec_inputs()

    def _L0_rec_setup():
        import jax, jax.numpy as jnp
        import numpy as np
        B, F, D = (512, 32, 32)
        LAYER_SIZE = [128, 128]

        def _cin_forward(inputs, filters):
            x0 = inputs
            prev = inputs
            outs = []
            for W in filters:
                z = jnp.einsum('bhd,bmd->bhmd', x0, prev)
                b, h, m, d = z.shape
                z = z.reshape(b, h * m, d)
                cur = jnp.einsum('bpd,pn->bnd', z, W[0])
                cur = jax.nn.relu(cur)
                prev = cur
                outs.append(cur)
            result = jnp.concatenate(outs, axis=1)
            return jnp.sum(result, axis=-1)
        key = jax.random.key(seed)
        k1, k2, k3 = jax.random.split(key, 3)
        inputs = jax.random.normal(k1, (B, F, D), dtype=jnp.float32)
        field_nums = [F] + LAYER_SIZE
        filter_0 = jax.random.normal(k2, (1, field_nums[0] * field_nums[0], field_nums[1]), dtype=jnp.float32) * 0.05
        filter_1 = jax.random.normal(k3, (1, field_nums[0] * field_nums[1], field_nums[2]), dtype=jnp.float32) * 0.05
        return {'inputs': inputs, 'filter_0': filter_0, 'filter_1': filter_1}
    _L0_rec_all = _L0_rec_setup()
    _L0_rec_in = {k: v for k, v in _L0_rec_all.items() if k in ('filter_0', 'filter_1')}
    del _L0_rec_all
    return {'dense_ctx': dense_ctx, 'ids': ids, 'tbl_0': tbl_0, 'tbl_1': tbl_1, 'tbl_2': tbl_2, 'tbl_3': tbl_3, 'tbl_4': tbl_4, 'tbl_5': tbl_5, 'tbl_6': tbl_6, 'tbl_7': tbl_7, 'tbl_8': tbl_8, 'tbl_9': tbl_9, 'tbl_10': tbl_10, 'tbl_11': tbl_11, 'tbl_12': tbl_12, 'tbl_13': tbl_13, 'tbl_14': tbl_14, 'tbl_15': tbl_15, 'tbl_16': tbl_16, 'tbl_17': tbl_17, 'tbl_18': tbl_18, 'tbl_19': tbl_19, 'tbl_20': tbl_20, 'tbl_21': tbl_21, 'tbl_22': tbl_22, 'tbl_23': tbl_23, 'tbl_24': tbl_24, 'tbl_25': tbl_25, 'tbl_26': tbl_26, 'tbl_27': tbl_27, 'tbl_28': tbl_28, 'tbl_29': tbl_29, 'tbl_30': tbl_30, 'tbl_31': tbl_31, 'W_top1': W_top1, 'b_top1': b_top1, 'W_top2': W_top2, 'b_top2': b_top2, 'W_top3': W_top3, 'L0_rec_filter_0': _L0_rec_in['filter_0'], 'L0_rec_filter_1': _L0_rec_in['filter_1']}

def reference(dense_ctx, ids, tbl_0, tbl_1, tbl_2, tbl_3, tbl_4, tbl_5, tbl_6, tbl_7, tbl_8, tbl_9, tbl_10, tbl_11, tbl_12, tbl_13, tbl_14, tbl_15, tbl_16, tbl_17, tbl_18, tbl_19, tbl_20, tbl_21, tbl_22, tbl_23, tbl_24, tbl_25, tbl_26, tbl_27, tbl_28, tbl_29, tbl_30, tbl_31, W_top1, b_top1, W_top2, b_top2, W_top3, L0_rec_filter_0, L0_rec_filter_1):
    import jax
    import jax.numpy as jnp

    def _L0_rec_ref(inputs, filter_0, filter_1):
        import jax, jax.numpy as jnp
        import numpy as np
        B, F, D = (512, 32, 32)
        LAYER_SIZE = [128, 128]

        def _cin_forward(inputs, filters):
            x0 = inputs
            prev = inputs
            outs = []
            for W in filters:
                z = jnp.einsum('bhd,bmd->bhmd', x0, prev)
                b, h, m, d = z.shape
                z = z.reshape(b, h * m, d)
                cur = jnp.einsum('bpd,pn->bnd', z, W[0])
                cur = jax.nn.relu(cur)
                prev = cur
                outs.append(cur)
            result = jnp.concatenate(outs, axis=1)
            return jnp.sum(result, axis=-1)
        return _cin_forward(inputs, (filter_0, filter_1))
    e = jnp.stack([tbl_0[ids[:, 0]], tbl_1[ids[:, 1]], tbl_2[ids[:, 2]], tbl_3[ids[:, 3]], tbl_4[ids[:, 4]], tbl_5[ids[:, 5]], tbl_6[ids[:, 6]], tbl_7[ids[:, 7]], tbl_8[ids[:, 8]], tbl_9[ids[:, 9]], tbl_10[ids[:, 10]], tbl_11[ids[:, 11]], tbl_12[ids[:, 12]], tbl_13[ids[:, 13]], tbl_14[ids[:, 14]], tbl_15[ids[:, 15]], tbl_16[ids[:, 16]], tbl_17[ids[:, 17]], tbl_18[ids[:, 18]], tbl_19[ids[:, 19]], tbl_20[ids[:, 20]], tbl_21[ids[:, 21]], tbl_22[ids[:, 22]], tbl_23[ids[:, 23]], tbl_24[ids[:, 24]], tbl_25[ids[:, 25]], tbl_26[ids[:, 26]], tbl_27[ids[:, 27]], tbl_28[ids[:, 28]], tbl_29[ids[:, 29]], tbl_30[ids[:, 30]], tbl_31[ids[:, 31]]], axis=1)
    z = _L0_rec_ref(e, L0_rec_filter_0, L0_rec_filter_1)
    z = z.reshape(z.shape[0], -1)
    h = jnp.concatenate([z, dense_ctx], axis=1)
    h = jnp.maximum(h @ W_top1 + b_top1, 0.0)
    h = jnp.maximum(h @ W_top2 + b_top2, 0.0)
    y = h @ W_top3
    return y

_drawn_inputs = setup_inputs


def setup_inputs(seed=0):
    import zlib

    import numpy as np

    out = dict(_drawn_inputs(seed))
    spreads = {'b_top1': (0.0, 0.438), 'b_top2': (0.0, 0.435)}
    factors = {'tbl_0': 6.005,
     'tbl_1': 5.951,
     'tbl_2': 6.161,
     'tbl_3': 6.102,
     'tbl_4': 6.195,
     'tbl_5': 6.011,
     'tbl_6': 6.056,
     'tbl_7': 6.321,
     'tbl_8': 6.086,
     'tbl_9': 5.835,
     'tbl_10': 6.075,
     'tbl_11': 5.908,
     'tbl_12': 5.802,
     'tbl_13': 5.816,
     'tbl_14': 6.09,
     'tbl_15': 6.107,
     'tbl_16': 5.824,
     'tbl_17': 6.028,
     'tbl_18': 6.392,
     'tbl_19': 6.376,
     'tbl_20': 5.969,
     'tbl_21': 6.092,
     'tbl_22': 6.063,
     'tbl_23': 6.203,
     'tbl_24': 6.296,
     'tbl_25': 5.83,
     'tbl_26': 5.798,
     'tbl_27': 6.159,
     'tbl_28': 6.306,
     'tbl_29': 5.971,
     'tbl_30': 5.874,
     'tbl_31': 5.968,
     'L0_rec_filter_1': 8.0}
    for name, (base, spread) in spreads.items():
        noise = np.random.default_rng([zlib.crc32(name.encode()), seed]).standard_normal(out[name].shape)
        drawn = base * np.exp(spread * noise) if base else spread * noise
        out[name] = jnp.asarray(drawn.astype(out[name].dtype))
    for name, factor in factors.items():
        out[name] = (out[name] * factor).astype(out[name].dtype)
    return out
```

```python
from contextlib import ExitStack

import concourse.bass as bass
from concourse import mybir

ALU = mybir.AluOpType
ACT = mybir.ActivationFunctionType
AX = mybir.AxisListType
F32 = mybir.dt.float32
F32R = mybir.dt.float32r
I32 = mybir.dt.int32

P = 128
B = 1024
F = 32
D = 32
N = 128
BC = 32
COLS = BC * D
HALF = COLS // 2
NCH = B // BC
TILES = B // P
QS = P // BC
NJ = F // 4
NI = N // 32
U0 = 5
U1 = NJ * NI
ND = 16
H1, H2 = 512, 256
NZ = 4
NS = 4
NDMA = 16

WHOLE0 = (1, 3)
WHOLE1_J = (3, 7)
DVE0 = ()
DVE1_J = (1, 5)


class Unit:

    def __init__(self, n, layer, ahead, i, j, count):
        self.n, self.layer, self.ahead, self.i, self.j = n, layer, ahead, i, j
        whole = j in (WHOLE0 if layer == 0 else WHOLE1_J)
        self.split = not whole
        self.s = count["split"]
        self.pool = self.split and j not in (DVE0 if layer == 0 else DVE1_J)
        self.sub = count["pool" if self.pool else "dve"]
        if self.split:
            count["split"] += 1
            count["pool" if self.pool else "dve"] += 1


def order(count, n, groups):
    out = []
    for layer, ahead, i in groups:
        for j in range(U0 if layer == 0 else NJ):
            out.append(Unit(n, layer, ahead, i, j, count))
            n += 1
    return out


def build(nc, dense_ctx, ids, tables, W_top1, b_top1, W_top2, b_top2, W_top3, filter_0, filter_1, out):
    count = {"split": 0, "pool": 0, "dve": 0}
    first = order(count, 0, [(0, 0, 0), (1, 0, 0)])
    before_body = dict(count)
    sections = []
    n = len(first)
    for q in range(QS):
        if q == QS - 1:
            final = order(dict(count), n, [(1, 0, 1), (1, 0, 2), (1, 0, 3)])
        sections.append(order(count, n, [(1, 0, 1), (0, 1, 0), (1, 0, 2), (1, 0, 3), (1, 1, 0)]))
        n += len(sections[-1])
    PER = {k: count[k] - before_body[k] for k in count}
    PER["unit"] = n - len(first)
    assert PER["unit"] % NZ == 0 and PER["split"] % NS == 0
    units = first + [u for sec in sections for u in sec]
    splits = [u for u in units if u.split]
    units_end = units[:final[0].n] + final
    splits_end = [u for u in units_end if u.split]

    def body_sections(last):
        return sections[:-1] + [final] if last else sections

    def unit_before(u):
        return (units_end if u in final else units)[u.n - NZ]

    def split_before(u):
        return (splits_end if u in final else splits)[u.s - NS]

    whole0 = [j for j in range(U0) if j in WHOLE0]
    split0 = [j for j in range(U0) if j not in WHOLE0]
    whole1 = [(i, j) for i in range(NI) for j in range(NJ) if j in WHOLE1_J]
    split1 = [(i, j) for i in range(NI) for j in range(NJ) if j not in WHOLE1_J]
    whole_at = {(0, 0, j): k for k, j in enumerate(whole0)}
    whole_at.update({(1, i, j): len(whole0) + k for k, (i, j) in enumerate(whole1)})
    split_at = {(0, 0, j): k for k, j in enumerate(split0)}
    split_at.update({(1, i, j): len(split0) + k for k, (i, j) in enumerate(split1)})

    with ExitStack() as ctx:
        def sb(name, shape, dt=F32):
            return ctx.enter_context(nc.sbuf_tensor(name, shape, dt))

        def ps(name, shape):
            return ctx.enter_context(nc.psum_tensor(name, shape, F32))

        def sem(name):
            return ctx.enter_context(nc.semaphore(name))

        x_dram = nc.dram_tensor("x_dram", [TILES, 2 * F, P * D], F32)
        y_dram = nc.dram_tensor("y_dram", [2, N, COLS], F32)

        idx = sb("idx", [P, F], I32)
        rows = sb("rows", [P, 4, F, D])
        xb = sb("xb", [P, P, D])
        xs = [sb(f"xs{p}", [P, NJ, COLS]) for p in range(2)]
        yr = sb("yr", [P, NI, COLS])
        y0 = sb("y0", [P, COLS])
        z = sb("z", [P, NZ, COLS])
        zh = sb("zh", [P, NS, COLS], F32R)
        zl = sb("zl", [P, NS, COLS], F32R)
        w_whole = sb("w_whole", [P, len(whole_at), N])
        wh = sb("wh", [P, len(split_at), N], F32R)
        wl = sb("wl", [P, len(split_at), N], F32R)
        sum0 = sb("sum0", [P, B])
        sum1 = sb("sum1", [P, B])
        w3 = sb("w3", [P, H2 // P])
        b1 = sb("b1", [P, H1 // P])
        b2 = sb("b2", [P, H2 // P])
        ident = sb("ident", [P, P])
        y_out = sb("y_out", [P, TILES])

        w1_raw = yr[:, :, :].rearrange("p i (j n) -> p i j n", n=N)
        w0_raw = xs[1][:, 0:1, :].rearrange("p a (j n) -> p (a j) n", n=N)
        w0_swap = xs[1][:, 1:2, :].rearrange("p a (j n) -> p (a j) n", n=N)
        spare = rows[:, :, :, :].rearrange("p r f d -> p (r f d)")
        w1 = spare[:, 0:3 * H1].rearrange("p (k n) -> p k n", n=H1)
        w2 = spare[:, 3 * H1:3 * H1 + H1 // P * H2].rearrange("p (k n) -> p k n", n=H2)
        spare = spare[:, 3 * H1 + H1 // P * H2:]
        dense_t, dense, dense_turn = spare[:, 0:B], spare[:, B:B + P], spare[:, B + P:B + 2 * P]
        h1 = xs[0][:, 0:4, :]
        h2 = xs[0][:, 4:6, :]

        ps_t = ps("ps_t", [P, 2, HALF])
        ps_0 = ps("ps_0", [P, 2, HALF])
        ps_1 = [ps(f"ps_1{p}", [P, 2, HALF]) for p in range(2)]

        banks = [ps_t[:, 0, :], ps_t[:, 1, :], ps_0[:, 0, :], ps_0[:, 1, :],
                 ps_1[0][:, 0, :], ps_1[0][:, 1, :], ps_1[1][:, 0, :], ps_1[1][:, 1, :]]

        idx_loaded = sem("idx_loaded")
        gathered = sem("gathered")
        rows_copied = sem("rows_copied")
        t_filled = sem("t_filled")
        t_copied = sem("t_copied")
        x_written = sem("x_written")
        xs_low = [sem(f"xs_low{p}") for p in range(2)]
        xs_high = [sem(f"xs_high{p}") for p in range(2)]
        yr_loaded = [sem(f"yr_loaded{i}") for i in range(NI)]
        y_written = sem("y_written")
        z_made = sem("z_made")
        zh_made = sem("zh_made")
        zl_dve = sem("zl_dve")
        zl_pool = sem("zl_pool")
        unit_done = sem("unit_done")
        y0_made = sem("y0_made")
        y1_made = sem("y1_made")
        sum0_made = sem("sum0_made")
        ps_1_free = sem("ps_1_free")
        consts_made = sem("consts_made")
        ident_zero = sem("ident_zero")
        zeros_made = sem("zeros_made")
        w0_loaded = sem("w0_loaded")
        w1_loaded = sem("w1_loaded")
        mlp_loaded = sem("mlp_loaded")
        dense_loaded = sem("dense_loaded")
        w0_summed = sem("w0_summed")
        wh_made = sem("wh_made")
        w_ready = sem("w_ready")
        dense_turned = sem("dense_turned")
        dense_copied = sem("dense_copied")
        dense_ready = sem("dense_ready")
        h1_filled = sem("h1_filled")
        h1_made = sem("h1_made")
        h2_filled = sem("h2_filled")
        h2_made = sem("h2_made")
        out_filled = sem("out_filled")
        out_made = sem("out_made")
        out_written = sem("out_written")

        def units_by(t, k):
            return PER["unit"] * t + k + 1

        def wait_zl(eng, t, u):
            if u.pool:
                eng.wait_ge(zl_pool, PER["pool"] * t + u.sub + 1)
            else:
                eng.wait_ge(zl_dve, PER["dve"] * t + u.sub + 1)

        def last_of(section, layer, i):
            return max(u.n for u in section if u.layer == layer and u.i == i)

        n_small = 0

        def filter_loads():
            f0 = filter_0[0]
            f1 = filter_1[0]
            loads0, loads1 = [], []
            for shift in range(17):
                j, s = shift // 4, shift % 4
                for lo, hi, wrap in ((0, F - shift, 0), (F - shift, F, F)):
                    if hi <= lo:
                        continue
                    part = slice(32 * s + lo, 32 * s + hi)
                    k = hi - lo
                    r = lo * 33 + shift - wrap
                    loads0.append((w0_raw[part, j, :], f0[r:r + 33 * (k - 1) + 1:33, :]))
                    if 0 < shift < 16:
                        r = lo * 33 + 32 * (shift - wrap)
                        loads0.append((w0_swap[part, j, :], f0[r:r + 33 * (k - 1) + 1:33, :]))
            for shift in range(F):
                j, s = shift // 4, shift % 4
                for lo, hi, wrap in ((0, F - shift, 0), (F - shift, F, F)):
                    if hi <= lo:
                        continue
                    part = slice(32 * s + lo, 32 * s + hi)
                    k = hi - lo
                    r = lo * 129 + 128 * (shift - wrap)
                    src = bass.AP(f1.tensor, f1.offset + r * N, [[129 * N, k], [32 * N, NI], [1, N]])
                    loads1.append((w1_raw[part, :, j, :], src))
            return loads0, loads1

        loads0, loads1 = filter_loads()

        block = ctx.enter_context(nc.Block())

        @block.sync
        def _(sp):
            def load_idx(t):
                sp.dma_start(idx[:, :], ids[bass.ds(t * P, P), :]).then_inc(idx_loaded, NDMA)

            def store_x(t):
                sp.wait_ge(t_copied, NJ * (t + 1))
                sp.dma_start(x_dram[t], xb[0:2 * F, :, :].rearrange("p b d -> p (b d)")).then_inc(x_written, NDMA)

            def load_xs(t, q, c_mod):
                p = c_mod % 2
                src = x_dram[t, 0:1, q * COLS:(q + 1) * COLS]
                for j0, j1, loaded in ((0, U0, xs_low[p]), (U0, NJ, xs_high[p])):
                    for s in range(4):
                        shifted = bass.AP(src.tensor, src.offset + (4 * j0 + s) * P * D,
                                          [[P * D, F], [4 * P * D, j1 - j0], [1, COLS]])
                        sp.dma_start(xs[p][32 * s:32 * s + 32, j0:j1, :], shifted).then_inc(loaded, NDMA)

            def store_y(c, p):
                sp.wait_ge(y0_made, c + 1)
                sp.dma_start(y_dram[p], y0[:, :]).then_inc(y_written, NDMA)

            def load_yr(i, p):
                for s in range(4):
                    sp.dma_start(yr[32 * s:32 * s + 32, i, :], y_dram[p, 32 * i:32 * i + 32, :]).then_inc(
                        yr_loaded[i], NDMA)

            load_idx(0)
            sp.wait_ge(zeros_made, 1)
            for dst, src in loads0:
                sp.dma_start(dst, src).then_inc(w0_loaded, NDMA)
            store_x(0)
            sp.wait_ge(x_written, NDMA)
            load_xs(0, 0, 0)
            sp.wait_ge(w_ready, 1)
            load_xs(0, 1, 1)
            store_y(0, 0)
            sp.wait_ge(y_written, NDMA)
            for i in range(NI):
                load_yr(i, 0)

            def load_perceptron():
                sp.wait_ge(t_filled, NJ * TILES)
                sp.dma_start(dense.rearrange("p (k c) -> p k c", c=ND),
                             dense_ctx.rearrange("(k p) c -> p k c", p=P)).then_inc(dense_loaded, NDMA)
                sp.wait_ge(zeros_made, 2)
                sp.dma_start(w1[:, 0:2, :],
                             W_top1[0:2 * P, :].rearrange("(k p) n -> p k n", p=P)).then_inc(mlp_loaded, NDMA)
                sp.dma_start(w1[0:ND, 2, :], W_top1[2 * P:2 * P + ND, :]).then_inc(mlp_loaded, NDMA)
                sp.dma_start(w2, W_top2.rearrange("(k p) n -> p k n", p=P)).then_inc(mlp_loaded, NDMA)
                sp.dma_start(w3[:, :], W_top3.rearrange("(k p) a -> p (k a)", p=P),
                             allow_slow_non_contiguous=True).then_inc(mlp_loaded, NDMA)
                sp.dma_start(b1[:, :], b_top1.rearrange("(k p) -> p k", p=P),
                             allow_slow_non_contiguous=True).then_inc(mlp_loaded, NDMA)
                sp.dma_start(b2[:, :], b_top2.rearrange("(k p) -> p k", p=P),
                             allow_slow_non_contiguous=True).then_inc(mlp_loaded, NDMA)

            def body(t, last):
                if last:
                    load_perceptron()
                for q in range(QS):
                    sec = body_sections(last)[q]
                    c = QS * t + q
                    more1 = not (last and q == QS - 1)
                    more2 = not (last and q >= QS - 2)
                    if q == 0 and not last:
                        sp.wait_ge(gathered, NDMA * F * (t + 1))
                        load_idx(t + 1)
                    if more1:
                        store_y(c + 1, (q + 1) % 2)
                        sp.wait_ge(y_written, NDMA * (c + 2))
                        load_yr(0, (q + 1) % 2)
                        sp.wait_ge(z_made, units_by(t, last_of(sec, 1, 1)))
                        load_yr(1, (q + 1) % 2)
                        sp.wait_ge(z_made, units_by(t, last_of(sec, 1, 2)))
                        load_yr(2, (q + 1) % 2)
                        if q == QS - 2 and not last:
                            store_x(t + 1)
                        sp.wait_ge(z_made, units_by(t, last_of(sec, 1, 3)))
                        load_yr(3, (q + 1) % 2)
                    if more2:
                        if q < QS - 2:
                            load_xs(t, q + 2, q)
                        else:
                            sp.wait_ge(x_written, NDMA * (t + 2))
                            load_xs(t + 1, q + 2 - QS, q)

            with sp.Fori(0, TILES - 1) as t:
                body(t, False)
            body(TILES - 1, True)
            sp.wait_ge(out_made, 1)
            sp.dma_start(out.rearrange("(p k) a -> p (k a)", k=TILES), y_out[:, :]).then_inc(out_written, NDMA)
            sp.wait_ge(out_written, NDMA)

        @block.gpsimd
        def _(pool):
            def gather(t, f):
                nc.gpsimd.indirect_dma_start(
                    out=rows[:, 0, f, :], out_offset=None, in_=tables[f][:, :],
                    in_offset=bass.IndirectOffsetOnAxis(ap=idx[:, 0 + f:f + 1], axis=0)).then_inc(gathered, NDMA)

            def low_part(t, u):
                pool.wait_ge(zh_made, PER["split"] * t + u.s + 1)
                if u.s >= NS:
                    pool.wait_ge(unit_done, units_by(t, split_before(u).n))
                nc.gpsimd.tensor_tensor(zl[:, u.s % NS, :], z[:, u.n % NZ, :], zh[:, u.s % NS, :].bitcast(F32),
                                        ALU.subtract).then_inc(zl_pool, 1)

            nc.gpsimd.memset(ident[:, :], 0.0).then_inc(ident_zero, 1)
            pool.wait_ge(ident_zero, 1)
            nc.gpsimd.affine_select(out=ident[:, :], in_=ident[:, :], compare_op=ALU.not_equal, fill=1.0, base=0,
                                    pattern=[[-1, P]], channel_multiplier=1).then_inc(consts_made, 1)
            pool.wait_ge(idx_loaded, NDMA)
            for f in range(F):
                gather(0, f)
            for u in first:
                if u.split and u.pool:
                    low_part(0, u)

            def body(t, last):
                f = 0
                for q in range(QS):
                    for u in body_sections(last)[q]:
                        if u.split and u.pool:
                            if f == 0 and not last:
                                pool.wait_ge(idx_loaded, NDMA * (t + 2))
                                pool.wait_ge(t_filled, NJ * (t + 1))
                            low_part(t, u)
                            if f < F and not last:
                                gather(t + 1, f)
                                f += 1
                assert last or f == F

            with pool.Fori(0, TILES - 1) as t:
                body(t, False)
            body(TILES - 1, True)

        @block.scalar
        def _(act):
            def high_part(t, u):
                act.wait_ge(z_made, units_by(t, u.n))
                if u.s >= NS:
                    act.wait_ge(unit_done, units_by(t, split_before(u).n))
                nc.scalar.activation(zh[:, u.s % NS, :], z[:, u.n % NZ, :], ACT.Copy).then_inc(zh_made, 1)

            def copy_rows(t):
                act.wait_ge(gathered, NDMA * F * (t + 1))
                if not (isinstance(t, int) and t == 0):
                    act.wait_ge(t_filled, NJ * t)
                four = rows[:, :, :, :].rearrange("p r f d -> p r (f d)")
                nc.scalar.activation(four[:, 1:4, :], four[:, 0:1, :].broadcast_to((P, 3, F * D)),
                                     ACT.Copy).then_inc(rows_copied, 1)

            def copy_x(t):
                for k in range(NJ):
                    act.wait_ge(t_filled, NJ * t + k + 1)
                    nc.scalar.activation(
                        xb[:, :, 4 * k:4 * k + 4].rearrange("p b d -> p d b"),
                        ps_t[:, k % 2, :].rearrange("p (d b) -> p d b", d=4), ACT.Copy).then_inc(t_copied, 1)

            def copy_dense():
                act.wait_ge(dense_turned, 1)
                nc.scalar.activation(dense_turn, ps_t[:, 1, 0:P], ACT.Copy).then_inc(dense_copied, 1)
                act.wait_ge(dense_copied, 1)
                act.wait_ge(zeros_made, 2)
                for k in range(TILES):
                    act.dma_start(dense_t[0:ND, k * P:(k + 1) * P], dense_turn[ND * k:ND * k + ND, :]).then_inc(
                        dense_ready, NDMA)

            def relu_0(t, c, u):
                act.wait_ge(unit_done, units_by(t, u.n))
                nc.scalar.activation(y0[:, :], ps_0[:, :, :].rearrange("p a n -> p (a n)"),
                                     ACT.Relu).then_inc(y0_made, 1)

            def relu_1(t, c_mod, u):
                act.wait_ge(unit_done, units_by(t, u.n))
                at = ps_1[c_mod % 2][:, :, :].rearrange("p a n -> p (a n)")
                nc.scalar.activation(at, at, ACT.Relu).then_inc(y1_made, 1)

            for dst, src in loads1:
                act.dma_start(dst, src).then_inc(w1_loaded, NDMA)

            act.wait_ge(w0_summed, 1)
            for j in split0:
                nc.scalar.activation(wh[:, split_at[0, 0, j], :], w0_raw[:, j, :], ACT.Copy).then_inc(wh_made, 1)
            act.wait_ge(w1_loaded, NDMA * len(loads1))
            for i, j in split1:
                nc.scalar.activation(wh[:, split_at[1, i, j], :], w1_raw[:, i, j, :], ACT.Copy).then_inc(wh_made, 1)
            copy_rows(0)
            copy_x(0)

            def run(t, todo, pending):
                for u, step in todo:
                    if u.split:
                        high_part(t, u)
                        for p in pending:
                            p[0] -= 1
                        while pending and pending[0][0] <= 0:
                            pending.pop(0)[1]()
                    if step:
                        pending.append([NS, step])

            run(0, [(u, None) for u in first if u.layer == 0], [])
            relu_0(0, 0, first[U0 - 1])
            run(0, [(u, None) for u in first if u.layer == 1], [])

            def body(t, last):
                pending = []
                for q in range(QS):
                    sec = body_sections(last)[q]
                    todo = []
                    for u in sec:
                        step = None
                        if u.layer == 0 and u.j == U0 - 1:
                            step = lambda v=u, c=QS * t + q + 1: relu_0(t, c, v)
                        elif u.n == last_of(sec, 1, 3):
                            step = lambda v=u, m=q: relu_1(t, m, v)
                        elif q == QS - 2 and not last and u.n == last_of(sec, 1, 2):
                            step = lambda: copy_x(t + 1)
                        elif q == 0 and last and u.n == last_of(sec, 1, 2):
                            step = copy_dense
                        todo.append((u, step))
                    if q == QS - 2 and not last:
                        copy_rows(t + 1)
                    run(t, todo, pending)
                assert last or not pending
                for p in pending:
                    p[1]()

            with act.Fori(0, TILES - 1) as t:
                body(t, False)
            body(TILES - 1, True)

            act.wait_ge(mlp_loaded, 6 * NDMA)
            act.wait_ge(z_made, units_by(TILES - 1, last_of(final, 1, 3)))
            for g in range(8):
                m, half = g % 4, g // 4
                act.wait_ge(h1_filled, g + 1)
                nc.scalar.activation(h1[:, m, half * HALF:(half + 1) * HALF], banks[g], ACT.Relu,
                                     bias=b1[:, m:m + 1]).then_inc(h1_made, 1)
            for g in range(4):
                m, half = g % 2, g // 2
                act.wait_ge(h2_filled, g + 1)
                nc.scalar.activation(h2[:, m, half * HALF:(half + 1) * HALF], banks[g], ACT.Relu,
                                     bias=b2[:, m:m + 1]).then_inc(h2_made, 1)
            act.wait_ge(out_filled, 1)
            nc.scalar.activation(y_out[:, :], banks[5][:, 0:TILES], ACT.Copy).then_inc(out_made, 1)

        @block.vector
        def _(dve):
            def product(t, u, q):
                p = (q + u.ahead) % 2
                xs_count = (QS * t + q + u.ahead) // 2 + 1 if isinstance(t, int) else 2 * t + (q + u.ahead) // 2 + 1
                if u.layer == 0 and u.j == 0:
                    dve.wait_ge(xs_low[p], 4 * NDMA * xs_count)
                    if (q + u.ahead) % QS == 0:
                        dve.wait_ge(t_copied, NJ * (t + (q + u.ahead) // QS + 1))
                if u.layer == 1 and u.j == 0:
                    dve.wait_ge(yr_loaded[u.i], 4 * NDMA * (QS * t + q + u.ahead + 1))
                if u.layer == 1 and u.i == 0 and u.j == U0:
                    dve.wait_ge(xs_high[p], 4 * NDMA * xs_count)
                if u.n >= NZ:
                    v = unit_before(u)
                    if v.split:
                        wait_zl(dve, t, v)
                    else:
                        dve.wait_ge(unit_done, units_by(t, v.n))
                if u.layer == 0:
                    b0 = (q + u.ahead) % QS * BC
                    other = xb[:, b0:b0 + BC, :].rearrange("p b d -> p (b d)")
                else:
                    other = yr[:, u.i, :]
                nc.vector.tensor_tensor(z[:, u.n % NZ, :], xs[p][:, u.j, :], other, ALU.mult).then_inc(z_made, 1)

            def low_part(t, u):
                dve.wait_ge(zh_made, PER["split"] * t + u.s + 1)
                if u.s >= NS:
                    dve.wait_ge(unit_done, units_by(t, split_before(u).n))
                nc.vector.tensor_tensor(zl[:, u.s % NS, :], z[:, u.n % NZ, :], zh[:, u.s % NS, :].bitcast(F32),
                                        ALU.subtract).then_inc(zl_dve, 1)

            def sum_0(t, c):
                dve.wait_ge(y0_made, c + 1)
                nc.vector.tensor_reduce(sum0[:, bass.ds(c * BC, BC)], y0[:, :].rearrange("p (b d) -> p b d", d=D),
                                        AX.X, ALU.add).then_inc(sum0_made, 1)

            def sum_1(t, c, q):
                dve.wait_ge(y1_made, c + 1)
                nc.vector.tensor_reduce(sum1[:, bass.ds(c * BC, BC)],
                                        ps_1[q % 2][:, :, :].rearrange("p a (b d) -> p (a b) d", d=D),
                                        AX.X, ALU.add).then_inc(ps_1_free, 1)

            def run(t, units, q, lagging):
                for u in units:
                    product(t, u, q)
                    while lagging and u.n - lagging[0].n >= 2:
                        low_part(t, lagging.pop(0))
                    if u.split and not u.pool:
                        lagging.append(u)

            nc.vector.memset(w0_raw[:, U0 - 1, :], 0.0)
            nc.vector.memset(w0_swap[:, 0, :], 0.0).then_inc(zeros_made, 1)
            nc.vector.memset(y_out[:, :], 0.0).then_inc(ps_1_free, 2)
            dve.wait_ge(w0_loaded, NDMA * len(loads0))
            nc.vector.tensor_tensor(w0_raw[:, 0:4, :], w0_raw[:, 0:4, :], w0_swap[:, 0:4, :],
                                    ALU.add).then_inc(w0_summed, 1)
            dve.wait_ge(w0_summed, 1)
            for j in whole0:
                nc.vector.tensor_copy(w_whole[:, whole_at[0, 0, j], :], w0_raw[:, j, :])
            for j in split0:
                k = split_at[0, 0, j]
                dve.wait_ge(wh_made, k + 1)
                nc.vector.tensor_tensor(wl[:, k, :], w0_raw[:, j, :], wh[:, k, :].bitcast(F32), ALU.subtract)
            dve.wait_ge(w1_loaded, NDMA * len(loads1))
            for i, j in whole1:
                nc.vector.tensor_copy(w_whole[:, whole_at[1, i, j], :], w1_raw[:, i, j, :])
            for i, j in split1:
                k = split_at[1, i, j]
                dve.wait_ge(wh_made, k + 1)
                ins = nc.vector.tensor_tensor(wl[:, k, :], w1_raw[:, i, j, :], wh[:, k, :].bitcast(F32), ALU.subtract)
            ins.then_inc(w_ready, 1)

            def flush(t, lagging):
                while lagging:
                    low_part(t, lagging.pop(0))

            lagging = []
            run(0, [u for u in first if u.layer == 0], 0, lagging)
            run(0, [u for u in first if u.layer == 1][:2], 0, lagging)
            run(0, [u for u in first if u.layer == 1][2:], 0, lagging)
            flush(0, lagging)
            sum_0(0, 0)

            def body(t, last):
                if last:
                    dve.wait_ge(t_filled, NJ * TILES)
                    nc.vector.memset(w1[:, 2, :], 0.0)
                    nc.vector.memset(dense_t, 0.0).then_inc(zeros_made, 1)
                lagging = []
                for q in range(QS):
                    c = QS * t + q
                    sec = body_sections(last)[q]
                    for u in sec:
                        run(t, [u], q, lagging)
                        if u.n == last_of(sec, 1, 2) and not (last and q == QS - 1):
                            sum_0(t, c + 1)
                        if u.layer == 1 and u.ahead and u.j == NJ - 1:
                            sum_1(t, c, q)
                flush(t, lagging)
                if last:
                    sum_1(t, QS * t + QS - 1, QS - 1)

            with dve.Fori(0, TILES - 1) as t:
                body(t, False)
            body(TILES - 1, True)

        @block.tensor
        def _(pe):
            def transpose_x(t):
                pe.wait_ge(rows_copied, t + 1)
                for k in range(NJ):
                    if not (isinstance(t, int) and t == 0 and k < 2):
                        pe.wait_ge(t_copied, NJ * t + k - 1)
                    for e in range(4):
                        d = 4 * k + e
                        ins = nc.tensor.matmul(ps_t[:, k % 2, e * P:(e + 1) * P],
                                               rows[:, :, :, d].rearrange("p r f -> p (r f)"), ident[:, :],
                                               start=True, stop=True, is_transpose=True)
                    ins.then_inc(t_filled, 1)

            def unit(t, u, q):
                c_ahead = q + u.ahead
                at = ps_0 if u.layer == 0 else ps_1[c_ahead % 2]
                begins = u.j == 0 and u.i == 0
                ends = u.j == U0 - 1 if u.layer == 0 else (u.j == NJ - 1 and u.i == NI - 1)
                if begins and u.layer == 0 and not (u.n == 0):
                    pe.wait_ge(y0_made, QS * t + c_ahead)
                if begins and u.layer == 1:
                    pe.wait_ge(ps_1_free, QS * t + c_ahead + 1)
                if not u.split:
                    pe.wait_ge(z_made, units_by(t, u.n))
                    k = whole_at[u.layer, u.i, u.j]
                    for half in range(2):
                        ins = nc.tensor.matmul(at[:, half, :], w_whole[:, k, :],
                                               z[:, u.n % NZ, half * HALF:(half + 1) * HALF],
                                               start=begins, stop=ends)
                else:
                    pe.wait_ge(zh_made, PER["split"] * t + u.s + 1)
                    k = split_at[u.layer, u.i, u.j]
                    r = u.s % NS
                    for w, x, part in ((wh, zh, 0), (wl, zh, 1), (wh, zl, 2)):
                        if part == 2:
                            wait_zl(pe, t, u)
                        for half in range(2):
                            ins = nc.tensor.matmul(at[:, half, :], w[:, k, :], x[:, r, half * HALF:(half + 1) * HALF],
                                                   start=begins and part == 0, stop=ends and part == 2)
                ins.then_inc(unit_done, 1)

            pe.wait_ge(consts_made, 1)
            transpose_x(0)
            pe.wait_ge(w_ready, 1)
            for u in first:
                unit(0, u, 0)

            def body(t, last):
                for q in range(QS):
                    sec = body_sections(last)[q]
                    for u in sec:
                        unit(t, u, q)
                        if q == QS - 2 and not last and u.n == last_of(sec, 1, 2):
                            transpose_x(t + 1)
                        if q == 0 and last and u.n == last_of(sec, 1, 2):
                            pe.wait_ge(dense_loaded, NDMA)
                            nc.tensor.matmul(ps_t[:, 1, 0:P], dense, ident[:, :], start=True, stop=True,
                                             is_transpose=True).then_inc(dense_turned, 1)

            with pe.Fori(0, TILES - 1) as t:
                body(t, False)
            body(TILES - 1, True)

            pe.wait_ge(mlp_loaded, 6 * NDMA)
            pe.wait_ge(dense_ready, TILES * NDMA)
            pe.wait_ge(sum0_made, NCH)
            for g in range(8):
                m, half = g % 4, g // 4
                cols = slice(half * HALF, (half + 1) * HALF)
                if g in (0, 6):
                    pe.wait_ge(ps_1_free, NCH + 2)
                for k, x in ((2, dense_t), (0, sum0), (1, sum1)):
                    ins = nc.tensor.matmul(banks[g], w1[:, k, m * P:(m + 1) * P], x[:, cols],
                                           start=k == 2, stop=k == 1)
                ins.then_inc(h1_filled, 1)
            for g in range(4):
                m, half = g % 2, g // 2
                pe.wait_ge(h1_made, 4 * half + 4)
                for k in range(H1 // P):
                    ins = nc.tensor.matmul(banks[g], w2[:, k, m * P:(m + 1) * P],
                                           h1[:, k, half * HALF:(half + 1) * HALF],
                                           start=k == 0, stop=k == H1 // P - 1)
                ins.then_inc(h2_filled, 1)
            pe.wait_ge(h2_made, 4)
            pe.wait_ge(h1_made, 8)
            for k in range(TILES):
                for m in range(H2 // P):
                    ins = nc.tensor.matmul(banks[5][:, k:k + 1], h2[:, m, k:B:TILES], w3[:, m:m + 1],
                                           start=m == 0, stop=m == H2 // P - 1)
            ins.then_inc(out_filled, 1)


_TABLES = [f"tbl_{f}" for f in range(F)]
_INS = (["dense_ctx", "ids"] + _TABLES
        + ["W_top1", "b_top1", "W_top2", "b_top2", "W_top3", "L0_rec_filter_0", "L0_rec_filter_1"])


def kernel(**inputs):
    import numpy as np
    from concourse import bacc
    from concourse.bass_utils import run_bass_kernel_spmd

    nc = bacc.Bacc("TRN2", target_bir_lowering=False, num_devices=1)
    arrays, aps = {}, {}
    for name in _INS:
        a = np.ascontiguousarray(inputs[name])
        arrays[f"in_{name}"] = a
        aps[name] = nc.dram_tensor(f"in_{name}", a.shape, mybir.dt.from_np(a.dtype), kind="ExternalInput").ap()
    out = nc.dram_tensor("out_y", (B, 1), F32, kind="ExternalOutput").ap()
    build(nc, aps["dense_ctx"], aps["ids"], [aps[k] for k in _TABLES], aps["W_top1"], aps["b_top1"],
          aps["W_top2"], aps["b_top2"], aps["W_top3"], aps["L0_rec_filter_0"], aps["L0_rec_filter_1"], out)
    r = run_bass_kernel_spmd(nc, [arrays], core_ids=[0])
    return r.results[0]["out_y"]
```

```python
from contextlib import ExitStack

import concourse.bass as bass
from concourse import mybir

ALU = mybir.AluOpType
ACT = mybir.ActivationFunctionType
AX = mybir.AxisListType
F32 = mybir.dt.float32
F32R = mybir.dt.float32r
I32 = mybir.dt.int32

P = 128
B = 1024
F = 32
D = 32
N = 128
ND = 16
H1, H2 = 512, 256
TILES = B // P
DC = 4
COLS = DC * P
QS = D // DC
NCH = TILES * QS
XROW = D * P
U0 = 5
NJ = F // 4
NI = N // 32
NZ = 8
NS = 7
NDMA = 16

WHOLE, POOL, DVE = "whole", "GpSimd", "VectorE"
KINDS_0 = (POOL, WHOLE, POOL)
KINDS_1 = (POOL, DVE, POOL, WHOLE)
DVE_LAG, ACT_LAG, LOW_LAG = 9, 5, 2
EARLY = 12


class Unit:

    def __init__(self, count, layer, ahead, js, i):
        self.layer, self.ahead, self.js, self.i = layer, ahead, js, i
        self.kind = KINDS_0[js[0] // 2] if layer == 0 else KINDS_1[i]
        self.split = self.kind != WHOLE
        self.n, self.s, self.low = count["unit"], count["split"], count[self.kind]
        count["unit"] += 1
        count["split"] += self.split
        count[self.kind] += 1


def section(count, more):
    one = [Unit(count, 1, 0, (0, 1), i) for i in range(NI)]
    if more:
        one += layer_0(count, 1)
    for j in range(2, NJ, 2):
        one += [Unit(count, 1, 0, (j, j + 1), i) for i in range(NI)]
    return one


def layer_0(count, ahead):
    return [Unit(count, 0, ahead, js, 0) for js in ((0, 1), (2, 3), (4,))]


def build(nc, dense_ctx, ids, tables, W_top1, b_top1, W_top2, b_top2, W_top3, filter_0, filter_1, out):
    START = {"unit": 0, "split": 0, WHOLE: 0, POOL: 0, DVE: 0}
    first = layer_0(START, 0)
    PER = {k: 0 for k in START}
    sections = [section(PER, True) for _ in range(QS)]
    ending = {k: 0 for k in START}
    last_sections = [section(ending, q < QS - 1) for q in range(QS)]
    tile_units = [u for sec in sections for u in sec]
    last_units = [u for sec in last_sections for u in sec]
    assert PER["unit"] % NZ == 0 and PER["split"] % NS == 0
    END0 = NI + 2
    HALF1 = NI + 3 + NI - 1
    SEC = len(sections[0])

    def before(t, u, back, splits):
        if u in first:
            return None
        here = last_units if isinstance(t, int) and t == TILES - 1 else tile_units
        if splits:
            here = [v for v in here if v.split]
        k = (u.s if splits else u.n) - back
        if k >= 0:
            return t, here[k]
        if isinstance(t, int) and t == 0:
            early = [v for v in first if v.split or not splits]
            return (None, early[k]) if -k <= len(early) else None
        here = [v for v in tile_units if v.split or not splits]
        return t - 1, here[k]

    def units_by(t, k):
        return k + 1 if t is None else START["unit"] + PER["unit"] * t + k + 1

    def splits_by(t, u):
        return u.s + 1 if t is None else START["split"] + PER["split"] * t + u.s + 1

    def lows_by(t, u):
        return u.low + 1 if t is None else START[u.kind] + PER[u.kind] * t + u.low + 1

    def body_sections(last):
        return last_sections if last else sections

    split0 = [j for j in range(U0) if KINDS_0[j // 2] != WHOLE]
    whole0 = [j for j in range(U0) if KINDS_0[j // 2] == WHOLE]
    split1 = [(j, i) for j in range(NJ) for i in range(NI) if KINDS_1[i] != WHOLE]
    whole1 = [(j, i) for j in range(NJ) for i in range(NI) if KINDS_1[i] == WHOLE]
    whole_at = {(0, j, 0): k for k, j in enumerate(whole0)}
    whole_at.update({(1, j, i): len(whole0) + k for k, (j, i) in enumerate(whole1)})
    split_at = {(0, j, 0): k for k, j in enumerate(split0)}
    split_at.update({(1, j, i): len(split0) + k for k, (j, i) in enumerate(split1)})

    with ExitStack() as ctx:
        def sb(name, shape, dt=F32):
            return ctx.enter_context(nc.sbuf_tensor(name, shape, dt))

        def ps(name, shape):
            return ctx.enter_context(nc.psum_tensor(name, shape, F32))

        def sem(name):
            return ctx.enter_context(nc.semaphore(name))

        x_dram = nc.dram_tensor("x_dram", [TILES, 2 * F, XROW], F32)
        y_dram = nc.dram_tensor("y_dram", [2, N, COLS], F32)

        f0_m = nc.dram_tensor("f0_m", [F, 2 * F, N], F32)
        f0_h = nc.dram_tensor("f0_h", [2 * F, F, N], F32)
        f1_h = nc.dram_tensor("f1_h", [2 * F, N, N], F32)

        idx = sb("idx", [P, F], I32)
        rows = sb("rows", [P, F * D])
        xt = sb("xt", [P, 2, COLS])
        xs = [sb(f"xs{p}", [P, NJ, COLS]) for p in range(2)]
        xp = [sb(f"xp{p}", [P, 1, COLS]) for p in range(2)]
        yr = [sb(f"yr{p}", [P, NI, COLS]) for p in range(2)]
        y0 = [sb(f"y0{p}", [P, COLS]) for p in range(2)]
        z = sb("z", [P, NZ, 2, COLS])
        zh = sb("zh", [P, NS, 2, COLS], F32R)
        zl = sb("zl", [P, NS, 2, COLS], F32R)
        w_whole = sb("w_whole", [P, len(whole_at), N])
        wh = sb("wh", [P, len(split_at), N], F32R)
        wl = sb("wl", [P, len(split_at), N], F32R)
        acc0 = sb("acc0", [P, COLS])
        acc1 = sb("acc1", [P, COLS])
        sum0 = sb("sum0", [P, P])
        sum1 = sb("sum1", [P, P])
        dense_t = sb("dense_t", [P, B])
        w1 = sb("w1", [P, 3, H1])
        w2 = sb("w2", [P, H1 // P, H2])
        w3 = sb("w3", [P, H2 // P])
        b1 = sb("b1", [P, H1 // P])
        b2 = sb("b2", [P, H2 // P])
        h1 = sb("h1", [P, H1 // P, P])
        h2 = sb("h2", [P, H2 // P, P])
        ident = sb("ident", [P, P])
        y_out = sb("y_out", [1, P])

        w1_raw = [yr[p][:, :, :].rearrange("p i (j n) -> p i j n", n=N) for p in range(2)]
        w0_raw = xs[1][:, 0:2, :].rearrange("p a (j n) -> p (a j) n", n=N)
        w0_swap = xs[1][:, 2:3, :].rearrange("p a (j n) -> p (a j) n", n=N)
        dense = xp[1][:, 0, 0:P]
        dense_turn = xp[1][:, 0, P:2 * P]

        ps_t = ps("ps_t", [P, 2, COLS])
        ps_0 = [ps(f"ps_0{p}", [P, COLS]) for p in range(2)]
        ps_1 = [ps(f"ps_1{p}", [P, COLS]) for p in range(2)]
        ps_h1 = ps("ps_h1", [P, COLS])
        ps_h2 = ps("ps_h2", [P, COLS])
        ps_y = ps_h2[0:1, H2:H2 + P]

        idx_loaded = sem("idx_loaded")
        gathered = sem("gathered")
        t_filled = sem("t_filled")
        t_copied = sem("t_copied")
        x_written = sem("x_written")
        xs_low = [sem(f"xs_low{p}") for p in range(2)]
        xs_high = [sem(f"xs_high{p}") for p in range(2)]
        xp_loaded = [sem(f"xp_loaded{p}") for p in range(2)]
        yr_loaded = [sem(f"yr_loaded{p}") for p in range(2)]
        y_written = sem("y_written")
        z_made = sem("z_made")
        zh_made = sem("zh_made")
        zl_made = {DVE: sem("zl_dve"), POOL: sem("zl_pool")}
        unit_done = sem("unit_done")
        y0_made = sem("y0_made")
        acc0_made = sem("acc0_made")
        acc1_made = sem("acc1_made")
        sum0_made = sem("sum0_made")
        sum1_made = sem("sum1_made")
        ident_zero = sem("ident_zero")
        ident_made = sem("ident_made")
        w0_zeros = sem("w0_zeros")
        pad_zeros = sem("pad_zeros")
        f0_doubled = sem("f0_doubled")
        f1_doubled = sem("f1_doubled")
        w0_loaded = sem("w0_loaded")
        w1_loaded = sem("w1_loaded")
        mlp_loaded = sem("mlp_loaded")
        dense_loaded = sem("dense_loaded")
        dense_turned = sem("dense_turned")
        dense_copied = sem("dense_copied")
        dense_ready = sem("dense_ready")
        w0_summed = sem("w0_summed")
        wh_made = sem("wh_made")
        w_ready = sem("w_ready")
        h1_filled = sem("h1_filled")
        h1_made = sem("h1_made")
        h2_filled = sem("h2_filled")
        h2_made = sem("h2_made")
        y_filled = sem("y_filled")
        y_made = sem("y_made")
        out_written = sem("out_written")

        def slot_n(t, u):
            return (u.n if t is None else START["unit"] + u.n) % NZ

        def slot_s(t, u):
            return (u.s if t is None else START["split"] + u.s) % NS

        def w0_load(s):
            src = f0_m[0:1, 0, :]
            rows_hm = bass.AP(src.tensor, src.offset + s * N, [[(2 * F + 1) * N, F], [4 * N, U0 if s == 0 else 4], [1, N]])
            src = f0_h[0:1, 0, :]
            j0 = 1 if s == 0 else 0
            rows_mh = bass.AP(src.tensor, src.offset + (4 * j0 + s) * F * N, [[(F + 1) * N, F], [4 * F * N, 4 - j0], [1, N]])
            part = slice(32 * s, 32 * s + 32)
            return (w0_raw[part, 0:(U0 if s == 0 else 4), :], rows_hm), (w0_swap[part, j0:4, :], rows_mh)

        def w1_load(s, half, i):
            src = f1_h[0:1, 0, :]
            of = bass.AP(src.tensor, src.offset + ((16 * half + s) * N + 32 * i) * N,
                         [[(N + 1) * N, F], [4 * N * N, 4], [1, N]])
            return w1_raw[half][32 * s:32 * s + 32, i, :, :], of

        block = ctx.enter_context(nc.Block())

        @block.sync
        def _(sp):
            def load_idx(t):
                sp.dma_start(idx[:, :], ids[bass.ds(t * P, P), :]).then_inc(idx_loaded, NDMA)

            def load_xs(t, q, j0, loaded):
                src = x_dram[t, 0:1, q * COLS:(q + 1) * COLS]
                for s in range(4):
                    shifted = bass.AP(src.tensor, src.offset + (4 * j0 + s) * XROW,
                                      [[XROW, F], [4 * XROW, NJ // 2], [1, COLS]])
                    sp.dma_start(xs[q % 2][32 * s:32 * s + 32, j0:j0 + NJ // 2, :], shifted).then_inc(
                        loaded[q % 2], NDMA)

            def load_xp(t, q):
                for s in range(4):
                    sp.dma_start(xp[q % 2][32 * s:32 * s + 32, 0, :],
                                 x_dram[t, 0:F, q * COLS:(q + 1) * COLS]).then_inc(xp_loaded[q % 2], NDMA)

            def load_yr(c, p):
                sp.wait_ge(y_written, NDMA * (c + 1))
                for s in range(4):
                    sp.dma_start(yr[p][32 * s:32 * s + 32, :, :],
                                 y_dram[p].rearrange("(i f) c -> f i c", f=32)).then_inc(yr_loaded[p], NDMA)

            load_idx(0)
            f0 = filter_0[0].rearrange("(h m) n -> h m n", m=F)
            for r in (0, F):
                sp.dma_start(f0_m[:, r:r + F, :], f0).then_inc(f0_doubled, NDMA)
                sp.dma_start(f0_h[r:r + F, :, :], f0).then_inc(f0_doubled, NDMA)
            sp.wait_ge(w0_zeros, 1)
            sp.wait_ge(f0_doubled, 4 * NDMA)
            for s in range(4):
                for dst, src in w0_load(s):
                    sp.dma_start(dst, src).then_inc(w0_loaded, NDMA)
            sp.wait_ge(x_written, 2 * NDMA)
            load_xp(0, 0)
            load_xs(0, 0, 0, xs_low)
            load_xs(0, 0, NJ // 2, xs_high)
            sp.wait_ge(w_ready, 1)
            sp.wait_ge(dense_ready, TILES * NDMA)
            load_xp(0, 1)
            load_xs(0, 1, 0, xs_low)
            load_xs(0, 1, NJ // 2, xs_high)
            load_yr(0, 0)
            sp.wait_ge(gathered, NDMA * F)
            load_idx(1)

            def body(t, zero, ahead, last):
                for q in range(QS):
                    c = QS * t + q
                    here = SEC * q
                    more1 = not (last and q == QS - 1)
                    more2 = not (last and q >= QS - 2)
                    if q == 5 and ahead:
                        sp.wait_ge(gathered, NDMA * F * (t + 2))
                        load_idx(t + 2)
                    if more1:
                        if not (zero and q == 0):
                            sp.wait_ge(z_made, units_by(t, here - 1))
                            load_xs(t if q < QS - 1 else t + 1, (q + 1) % QS, NJ // 2, xs_high)
                        load_yr(c + 1, (q + 1) % 2)
                    if more2:
                        sp.wait_ge(z_made, units_by(t, here + HALF1))
                        t2 = t if q < QS - 2 else t + 1
                        load_xp(t2, (q + 2) % QS)
                        load_xs(t2, (q + 2) % QS, 0, xs_low)

            body(0, True, True, False)
            with sp.Fori(1, TILES - 2) as t:
                body(t, False, True, False)
            body(TILES - 2, False, False, False)
            body(TILES - 1, False, False, True)
            sp.wait_ge(out_written, NDMA * TILES)

        @block.gpsimd
        def _(pool):
            def gather(f):
                nc.gpsimd.indirect_dma_start(
                    out=rows[:, f * D:(f + 1) * D], out_offset=None, in_=tables[f][:, :],
                    in_offset=bass.IndirectOffsetOnAxis(ap=idx[:, f:f + 1], axis=0)).then_inc(gathered, NDMA)

            def low_part(t, u):
                k = len(u.js)
                pool.wait_ge(zh_made, splits_by(t, u))
                old = before(t, u, NS, True)
                if old:
                    pool.wait_ge(unit_done, units_by(old[0], old[1].n))
                nc.gpsimd.tensor_tensor(zl[:, slot_s(t, u), 0:k, :], z[:, slot_n(t, u), 0:k, :],
                                        zh[:, slot_s(t, u), 0:k, :].bitcast(F32),
                                        ALU.subtract).then_inc(zl_made[POOL], 1)

            nc.gpsimd.memset(ident[:, :], 0.0).then_inc(ident_zero, 1)
            pool.wait_ge(ident_zero, 1)
            nc.gpsimd.affine_select(out=ident[:, :], in_=ident[:, :], compare_op=ALU.not_equal, fill=1.0, base=0,
                                    pattern=[[-1, P]], channel_multiplier=1).then_inc(ident_made, 1)
            pool.wait_ge(idx_loaded, NDMA)
            for f in range(F):
                gather(f)
            for u in first:
                if u.kind == POOL:
                    low_part(None, u)

            def body(t, zero, ahead, last):
                f = 0 if zero else EARLY
                for q in range(QS):
                    if q == 5:
                        assert last or f == F
                        f = 0
                    low = 0
                    for u in body_sections(last)[q]:
                        if u.kind != POOL:
                            continue
                        tile = 1 if q < 5 else 2
                        fetch = (not last if q < 5 else ahead) and f < (F if q < 5 else EARLY)
                        fetch = fetch and low in ((2, 3, 4, 5, 6, 7, 8) if zero and q < 5 else (2, 4, 7, 9))
                        if fetch and f == 0:
                            pool.wait_ge(idx_loaded, NDMA * (t + tile + 1))
                            pool.wait_ge(t_filled, t + tile)
                        low_part(t, u)
                        if fetch:
                            gather(f)
                            f += 1
                        low += 1

            body(0, True, True, False)
            with pool.Fori(1, TILES - 2) as t:
                body(t, False, True, False)
            body(TILES - 2, False, False, False)
            body(TILES - 1, False, False, True)

        @block.scalar
        def _(act):
            def high_part(t, u):
                k = len(u.js)
                act.wait_ge(z_made, units_by(t, u.n))
                old = before(t, u, NS, True)
                if old:
                    act.wait_ge(unit_done, units_by(old[0], old[1].n))
                nc.scalar.activation(zh[:, slot_s(t, u), 0:k, :], z[:, slot_n(t, u), 0:k, :],
                                     ACT.Copy).then_inc(zh_made, 1)

            def store_x(t):
                act.wait_ge(t_filled, t + 1)
                if not (isinstance(t, int) and t == 0):
                    act.wait_ge(x_written, 2 * NDMA * t)
                for k in range(2):
                    ins = nc.scalar.activation(xt[:, k, :], ps_t[:, k, :], ACT.Copy)
                ins.then_inc(t_copied, 1)
                act.wait_ge(t_copied, t + 1)
                for r in (0, F):
                    act.dma_start(x_dram[t, r:r + F, :].rearrange("f (g c) -> (f g) c", g=4),
                                  xt[:, :, :].rearrange("p a c -> p (a c)")).then_inc(x_written, NDMA)

            def relu_0(t, c, p, u, early):
                if not early:
                    act.wait_ge(acc0_made, c - 1)
                    act.wait_ge(y_written, NDMA * (c - 1))
                act.wait_ge(unit_done, units_by(t, u.n))
                nc.scalar.activation(y0[p][:, :], ps_0[p][:, :], ACT.Relu).then_inc(y0_made, 1)
                act.wait_ge(y0_made, c + 1)
                act.dma_start(y_dram[p], y0[p][:, :]).then_inc(y_written, NDMA)

            def relu_h1(t):
                act.wait_ge(h1_filled, t + 1)
                for m in range(H1 // P):
                    ins = nc.scalar.activation(h1[:, m, :], ps_h1[:, m * P:(m + 1) * P], ACT.Relu, bias=b1[:, m:m + 1])
                ins.then_inc(h1_made, 1)

            def relu_h2(t):
                act.wait_ge(h2_filled, t + 1)
                for m in range(H2 // P):
                    ins = nc.scalar.activation(h2[:, m, :], ps_h2[:, m * P:(m + 1) * P], ACT.Relu, bias=b2[:, m:m + 1])
                ins.then_inc(h2_made, 1)

            def store_y(t):
                if not (isinstance(t, int) and t == 0):
                    act.wait_ge(out_written, NDMA * t)
                act.wait_ge(y_filled, t + 1)
                nc.scalar.activation(y_out[:, :], ps_y, ACT.Copy).then_inc(y_made, 1)
                act.wait_ge(y_made, t + 1)
                act.dma_start(out[bass.ds(t * P, P), :].rearrange("b a -> a b"), y_out[:, :]).then_inc(out_written, NDMA)

            f1 = filter_1[0].rearrange("(h m) n -> h m n", m=N)
            for r in (0, F):
                act.dma_start(f1_h[r:r + F, :, :], f1).then_inc(f1_doubled, NDMA)
            act.dma_start(dense.rearrange("p (k c) -> p k c", c=ND),
                          dense_ctx.rearrange("(k p) c -> p k c", p=P)).then_inc(dense_loaded, NDMA)
            act.dma_start(w1[:, 0:2, :], W_top1[0:2 * P, :].rearrange("(k p) n -> p k n", p=P)).then_inc(mlp_loaded, NDMA)
            act.dma_start(w2[:, :, :], W_top2.rearrange("(k p) n -> p k n", p=P)).then_inc(mlp_loaded, NDMA)
            act.dma_start(w3[:, :], W_top3.rearrange("(k p) a -> p (k a)", p=P),
                          allow_slow_non_contiguous=True).then_inc(mlp_loaded, NDMA)
            act.dma_start(b1[:, :], b_top1.rearrange("(k p) -> p k", p=P),
                          allow_slow_non_contiguous=True).then_inc(mlp_loaded, NDMA)
            act.dma_start(b2[:, :], b_top2.rearrange("(k p) -> p k", p=P),
                          allow_slow_non_contiguous=True).then_inc(mlp_loaded, NDMA)
            act.wait_ge(f1_doubled, 2 * NDMA)
            for half in range(2):
                for s in range(4):
                    for i in range(NI):
                        dst, src = w1_load(s, half, i)
                        act.dma_start(dst, src).then_inc(w1_loaded, NDMA)
            act.wait_ge(pad_zeros, 1)
            act.dma_start(w1[0:ND, 2, :], W_top1[2 * P:2 * P + ND, :]).then_inc(mlp_loaded, NDMA)

            act.wait_ge(dense_turned, 1)
            nc.scalar.activation(dense_turn, ps_t[:, 1, 0:P], ACT.Copy).then_inc(dense_copied, 1)
            act.wait_ge(dense_copied, 1)
            for k in range(TILES):
                act.dma_start(dense_t[0:ND, k * P:(k + 1) * P], dense_turn[ND * k:ND * k + ND, :]).then_inc(
                    dense_ready, NDMA)
            act.wait_ge(w0_summed, 1)
            for j in split0:
                nc.scalar.activation(wh[:, split_at[0, j, 0], :], w0_raw[:, j, :], ACT.Copy).then_inc(wh_made, 1)
            act.wait_ge(w1_loaded, 8 * NI * NDMA)
            for j, i in split1:
                nc.scalar.activation(wh[:, split_at[1, j, i], :], w1_raw[j // 4][:, i, j % 4, :],
                                     ACT.Copy).then_inc(wh_made, 1)
            store_x(0)
            for u in first:
                if u.split:
                    high_part(None, u)
            relu_0(None, 0, 0, first[-1], True)

            def body(t, zero, last):
                for q in range(QS):
                    c = QS * t + q
                    for k, u in enumerate(body_sections(last)[q]):
                        if u.split:
                            high_part(t, u)
                        if k == END0 + ACT_LAG and not (last and q == QS - 1):
                            if q == QS - 2 and not last:
                                act.wait_ge(x_written, 2 * NDMA * (t + 2))
                            relu_0(t, c + 1, (q + 1) % 2, body_sections(last)[q][END0], zero and q == 0)
                        if q == 5 and k == 3 + ACT_LAG and not last:
                            store_x(t + 1)
                        if not zero:
                            if (q, k) == H1_RELU:
                                relu_h1(t - 1)
                            if (q, k) == H2_RELU:
                                relu_h2(t - 1)
                            if (q, k) == Y_COPY:
                                store_y(t - 1)

            body(0, True, False)
            with act.Fori(1, TILES - 1) as t:
                body(t, False, False)
            body(TILES - 1, False, True)
            relu_h1(TILES - 1)
            relu_h2(TILES - 1)
            store_y(TILES - 1)

        @block.vector
        def _(dve):
            def product(t, u, q):
                k = len(u.js)
                t1 = 0 if t is None else t
                c_mod = q + u.ahead
                p = c_mod % 2
                loads = 4 * NDMA * (QS // 2 * t1 + c_mod // 2 + 1)
                if u.layer == 0 and u.js[0] == 0:
                    dve.wait_ge(xp_loaded[p], loads)
                    dve.wait_ge(xs_low[p], loads)
                if u.layer == 0 and u.js[0] == 4:
                    dve.wait_ge(xs_high[p], loads)
                if u.layer == 1 and u.js[0] == 0 and u.i == 0:
                    dve.wait_ge(yr_loaded[p], loads)
                old = before(t, u, NZ, False)
                if old:
                    if old[1].split:
                        dve.wait_ge(zl_made[old[1].kind], lows_by(*old))
                    else:
                        dve.wait_ge(unit_done, units_by(old[0], old[1].n))
                other = xp[p][:, 0:1, :] if u.layer == 0 else yr[p][:, u.i:u.i + 1, :]
                nc.vector.tensor_tensor(z[:, slot_n(t, u), 0:k, :], xs[p][:, u.js[0]:u.js[0] + k, :],
                                        other.broadcast_to((P, k, COLS)), ALU.mult).then_inc(z_made, 1)

            def low_part(t, u):
                k = len(u.js)
                dve.wait_ge(zh_made, splits_by(t, u))
                old = before(t, u, NS, True)
                if old:
                    dve.wait_ge(unit_done, units_by(old[0], old[1].n))
                nc.vector.tensor_tensor(zl[:, slot_s(t, u), 0:k, :], z[:, slot_n(t, u), 0:k, :],
                                        zh[:, slot_s(t, u), 0:k, :].bitcast(F32),
                                        ALU.subtract).then_inc(zl_made[DVE], 1)

            def add_0(c, p, starts):
                dve.wait_ge(y0_made, c + 1)
                if starts:
                    nc.vector.tensor_copy(acc0[:, :], y0[p][:, :]).then_inc(acc0_made, 1)
                else:
                    dve.wait_ge(acc0_made, c)
                    nc.vector.tensor_tensor(acc0[:, :], acc0[:, :], y0[p][:, :], ALU.add).then_inc(acc0_made, 1)

            def add_1(t, c, p, end, starts):
                dve.wait_ge(unit_done, units_by(t, end))
                if starts:
                    nc.vector.tensor_scalar(acc1[:, :], ps_1[p][:, :], 0.0, None, ALU.max).then_inc(acc1_made, 1)
                else:
                    dve.wait_ge(acc1_made, c)
                    nc.vector.scalar_tensor_tensor(out=acc1[:, :], in0=ps_1[p][:, :], scalar=0.0, in1=acc1[:, :],
                                                   op0=ALU.max, op1=ALU.add).then_inc(acc1_made, 1)

            def finish_sum(t, acc, acc_made, total, total_made):
                dve.wait_ge(acc_made, QS * (t + 1))
                if not (isinstance(t, int) and t == 0):
                    dve.wait_ge(h1_filled, t)
                nc.vector.tensor_reduce(total[:, :], acc[:, :].rearrange("p (e b) -> p b e", b=P), AX.X,
                                        ALU.add).then_inc(total_made, 1)

            nc.vector.memset(w0_raw[:, U0 - 1, :], 0.0)
            nc.vector.memset(w0_swap[:, 0, :], 0.0).then_inc(w0_zeros, 1)
            nc.vector.memset(w1[:, 2, :], 0.0)
            nc.vector.memset(dense_t[:, :], 0.0).then_inc(pad_zeros, 1)
            dve.wait_ge(w0_loaded, 8 * NDMA)
            nc.vector.tensor_tensor(w0_raw[:, 0:4, :], w0_raw[:, 0:4, :], w0_swap[:, 0:4, :],
                                    ALU.add).then_inc(w0_summed, 1)
            dve.wait_ge(w0_summed, 1)
            for j in whole0:
                nc.vector.tensor_copy(w_whole[:, whole_at[0, j, 0], :], w0_raw[:, j, :])
            for j in split0:
                k = split_at[0, j, 0]
                dve.wait_ge(wh_made, k + 1)
                nc.vector.tensor_tensor(wl[:, k, :], w0_raw[:, j, :], wh[:, k, :].bitcast(F32), ALU.subtract)
            dve.wait_ge(w1_loaded, 8 * NI * NDMA)
            for j, i in whole1:
                nc.vector.tensor_copy(w_whole[:, whole_at[1, j, i], :], w1_raw[j // 4][:, i, j % 4, :])
            for j, i in split1:
                k = split_at[1, j, i]
                dve.wait_ge(wh_made, k + 1)
                ins = nc.vector.tensor_tensor(wl[:, k, :], w1_raw[j // 4][:, i, j % 4, :],
                                              wh[:, k, :].bitcast(F32), ALU.subtract)
            ins.then_inc(w_ready, 1)

            for u in first:
                product(None, u, 0)
            add_0(0, 0, True)

            def body(t, zero, last):
                waiting = []
                for q in range(QS):
                    c = QS * t + q
                    for k, u in enumerate(body_sections(last)[q]):
                        product(t, u, q)
                        while waiting and u.n - waiting[0].n >= LOW_LAG:
                            low_part(t, waiting.pop(0))
                        if u.kind == DVE:
                            waiting.append(u)
                        if k == DVE_LAG and not (zero and q == 0):
                            add_1(t, c - 1, (q + 1) % 2, SEC * q - 1, q == 1)
                            if q == 0:
                                finish_sum(t - 1, acc1, acc1_made, sum1, sum1_made)
                        if k == END0 + DVE_LAG and not (last and q == QS - 1):
                            add_0(c + 1, (q + 1) % 2, q == QS - 1)
                            if q == QS - 2:
                                finish_sum(t, acc0, acc0_made, sum0, sum0_made)
                while waiting:
                    low_part(t, waiting.pop(0))

            body(0, True, False)
            with dve.Fori(1, TILES - 1) as t:
                body(t, False, False)
            body(TILES - 1, False, True)
            add_1(TILES - 1, NCH - 1, 1, len(last_units) - 1, False)
            finish_sum(TILES - 1, acc1, acc1_made, sum1, sum1_made)

        @block.tensor
        def _(pe):
            def transpose_x(t):
                pe.wait_ge(gathered, NDMA * F * (t + 1))
                if not (isinstance(t, int) and t == 0):
                    pe.wait_ge(t_copied, t)
                for e in range(8):
                    ins = nc.tensor.matmul(ps_t[:, e // 4, e % 4 * P:(e % 4 + 1) * P], rows[:, e:F * D:8],
                                           ident[:, :], start=True, stop=True, is_transpose=True)
                ins.then_inc(t_filled, 1)

            def unit(t, u, q):
                c = (0 if t is None else QS * t) + q + u.ahead
                p = (q + u.ahead) % 2
                at = ps_0[p] if u.layer == 0 else ps_1[p]
                begins = u.js[0] == 0 and u.i == 0
                ends = u.js[-1] == U0 - 1 if u.layer == 0 else (u.js[-1] == NJ - 1 and u.i == NI - 1)
                early = (t is None or (isinstance(t, int) and t == 0)) and q + u.ahead < 2
                if begins and not early:
                    pe.wait_ge(y0_made if u.layer == 0 else acc1_made, c - 1)
                if not u.split:
                    pe.wait_ge(z_made, units_by(t, u.n))
                    for k, j in enumerate(u.js):
                        ins = nc.tensor.matmul(at[:, :], w_whole[:, whole_at[u.layer, j, u.i], :],
                                               z[:, slot_n(t, u), k, :],
                                               start=begins and k == 0, stop=ends and j == u.js[-1])
                else:
                    r = slot_s(t, u)
                    pe.wait_ge(zh_made, splits_by(t, u))
                    for k, j in enumerate(u.js):
                        w = split_at[u.layer, j, u.i]
                        nc.tensor.matmul(at[:, :], wh[:, w, :], zh[:, r, k, :], start=begins and k == 0, stop=False)
                        nc.tensor.matmul(at[:, :], wl[:, w, :], zh[:, r, k, :], start=False, stop=False)
                    pe.wait_ge(zl_made[u.kind], lows_by(t, u))
                    for k, j in enumerate(u.js):
                        w = split_at[u.layer, j, u.i]
                        ins = nc.tensor.matmul(at[:, :], wh[:, w, :], zl[:, r, k, :], start=False,
                                               stop=ends and j == u.js[-1])
                ins.then_inc(unit_done, 1)

            def perceptron_1(t):
                pe.wait_ge(sum0_made, t + 1)
                pe.wait_ge(sum1_made, t + 1)
                for m in range(H1 // P):
                    for k, x in ((0, sum0[:, :]), (1, sum1[:, :]), (2, dense_t[:, bass.ds(t * P, P)])):
                        ins = nc.tensor.matmul(ps_h1[:, m * P:(m + 1) * P], w1[:, k, m * P:(m + 1) * P], x,
                                               start=k == 0, stop=k == 2)
                ins.then_inc(h1_filled, 1)

            def perceptron_2(t):
                pe.wait_ge(h1_made, t + 1)
                for m in range(H2 // P):
                    for k in range(H1 // P):
                        ins = nc.tensor.matmul(ps_h2[:, m * P:(m + 1) * P], w2[:, k, m * P:(m + 1) * P], h1[:, k, :],
                                               start=k == 0, stop=k == H1 // P - 1)
                ins.then_inc(h2_filled, 1)

            def perceptron_3(t):
                pe.wait_ge(h2_made, t + 1)
                for k in range(H2 // P):
                    ins = nc.tensor.matmul(ps_y, w3[:, k:k + 1], h2[:, k, :], start=k == 0, stop=k == H2 // P - 1)
                ins.then_inc(y_filled, 1)

            pe.wait_ge(ident_made, 1)
            pe.wait_ge(dense_loaded, NDMA)
            nc.tensor.matmul(ps_t[:, 1, 0:P], dense, ident[:, :], start=True, stop=True,
                             is_transpose=True).then_inc(dense_turned, 1)
            pe.wait_ge(dense_copied, 1)
            transpose_x(0)
            pe.wait_ge(w_ready, 1)
            for u in first:
                unit(None, u, 0)

            def body(t, zero, last):
                if not zero:
                    pass
                for q in range(QS):
                    for k, u in enumerate(body_sections(last)[q]):
                        unit(t, u, q)
                        if q == 5 and k == 3 and not last:
                            transpose_x(t + 1)
                        if not zero:
                            if (q, k) == H1_MM:
                                perceptron_1(t - 1)
                            if (q, k) == H2_MM:
                                perceptron_2(t - 1)
                            if (q, k) == Y_MM:
                                perceptron_3(t - 1)

            body(0, True, False)
            pe.wait_ge(mlp_loaded, 6 * NDMA)
            pe.wait_ge(dense_ready, TILES * NDMA)
            with pe.Fori(1, TILES - 1) as t:
                body(t, False, False)
            body(TILES - 1, False, True)
            perceptron_1(TILES - 1)
            perceptron_2(TILES - 1)
            perceptron_3(TILES - 1)


H1_MM, H1_RELU = (0, 14), (1, 1)
H2_MM, H2_RELU = (1, 8), (1, 14)
Y_MM, Y_COPY = (2, 2), (2, 8)

_TABLES = [f"tbl_{f}" for f in range(F)]
_INS = (["dense_ctx", "ids"] + _TABLES
        + ["W_top1", "b_top1", "W_top2", "b_top2", "W_top3", "L0_rec_filter_0", "L0_rec_filter_1"])


def kernel(**inputs):
    import numpy as np
    from concourse import bacc
    from concourse.bass_utils import run_bass_kernel_spmd

    nc = bacc.Bacc("TRN2", target_bir_lowering=False, num_devices=1)
    arrays, aps = {}, {}
    for name in _INS:
        a = np.ascontiguousarray(inputs[name])
        arrays[f"in_{name}"] = a
        aps[name] = nc.dram_tensor(f"in_{name}", a.shape, mybir.dt.from_np(a.dtype), kind="ExternalInput").ap()
    out = nc.dram_tensor("out_y", (B, 1), F32, kind="ExternalOutput").ap()
    build(nc, aps["dense_ctx"], aps["ids"], [aps[k] for k in _TABLES], aps["W_top1"], aps["b_top1"],
          aps["W_top2"], aps["b_top2"], aps["W_top3"], aps["L0_rec_filter_0"], aps["L0_rec_filter_1"], out)
    r = run_bass_kernel_spmd(nc, [arrays], core_ids=[0])
    return r.results[0]["out_y"]
```

```python
from contextlib import ExitStack

import concourse.bass as bass
from concourse import mybir

ALU = mybir.AluOpType
ACT = mybir.ActivationFunctionType
AX = mybir.AxisListType
F32 = mybir.dt.float32
F32R = mybir.dt.float32r
I32 = mybir.dt.int32

P = 128
B = 1024
F = 32
D = 32
N = 128
ND = 16
H1, H2 = 512, 256
TILES = B // P
DC = 4
COLS = DC * P
QS = D // DC
NCH = TILES * QS
XROW = D * P
U0 = 5
UNITS = ((0, 1), (2, 3), (4,))
HB = COLS // N
NDMA = 16
X_LOADS = 6

TAKES = "ADAADADA"
A_BANKS = [k for k in range(8) if TAKES[k] == "A"]
D_BANKS = [k for k in range(8) if TAKES[k] == "D"]
NA, NV = len(A_BANKS), len(D_BANKS)
POOLED = (3, 3, 4, 4)
A_RING, D_RING = 4, 3
PAIR = [n * HB // 2 for n in POOLED]
FOLD = [n // 2 for n in PAIR]
A_AT = NV * HB
G_AT = [A_AT + (NA - n) * HB for n in POOLED]
PARTS = [g + n for g, n in zip(G_AT, FOLD)]

Z_AT = ((0, 0), (1, 0), (1, 5))
ZH_AT = ((0, 5), (1, 4), (2, 0))
MM_AT = ((2, 1), (2, 7), (3, 0))
YH_AT, YL_AT, ACC0_AT = (3, 1), (3, 1), (3, 1)
REDUCE_K = 6
RELU_AT = (1, 3)
POOL_STEPS = (("pair", 0), ("low", 0), ("fold", 0), ("gather", 0), ("pair", 1), ("low", 1), ("fold", 1),
              ("low", 2), ("gather", 1), ("pair", 2), ("gather", 2), ("fold", 2), ("gather", 3), ("gather", 4),
              ("pair", 3), ("gather", 5), ("fold", 3))
GATHERS = (6, 6, 4, 5, 6, 5, 0, 0)
T_MM, T_COPY = ((6, 0, 5), (6, 1, 1)), ((6, 0, 7), (6, 1, 4))
SUM0_AT, SUM1_AT = (QS - 1, 1, 4), (0, 1, 4)
TURN_MM, TURN_COPY = (0, 3, 6), (0, 3, 7)
H1_MM, H1_RELU = (1, 0, 5), (1, 1, 1)
H2_MM, H2_RELU = (1, 3, 6), (1, 3, 7)
Y_MM, Y_COPY = (2, 0, 3), (2, 0, 5)


def some(count):
    return not (isinstance(count, int) and count <= 0)


def build(nc, dense_ctx, ids, tables, W_top1, b_top1, W_top2, b_top2, W_top3, filter_0, filter_1, out):
    assert sum(GATHERS) == F and QS * DC * NA % A_RING == 0 and QS * DC * NV % D_RING == 0

    with ExitStack() as ctx:
        def sb(name, shape, dt=F32):
            return ctx.enter_context(nc.sbuf_tensor(name, shape, dt))

        def ps(name, shape):
            return ctx.enter_context(nc.psum_tensor(name, shape, F32))

        def sem(name):
            return ctx.enter_context(nc.semaphore(name))

        x_dram = nc.dram_tensor("x_dram", [TILES, 2 * F, XROW], F32)
        f0_m = nc.dram_tensor("f0_m", [F, 2 * F, N], F32)
        f0_h = nc.dram_tensor("f0_h", [2 * F, F, N], F32)

        idx = sb("idx", [P, F], I32)
        rows = [sb(f"rows{p}", [P, F * D]) for p in range(2)]
        xt = sb("xt", [P, 2, COLS])
        xs = [sb(f"xs{p}", [P, U0, COLS]) for p in range(2)]
        xp = [sb(f"xp{p}", [P, 1, COLS]) for p in range(2)]
        z = sb("z", [P, U0, COLS])
        zh = sb("zh", [P, U0, COLS], F32R)
        zl = sb("zl", [P, U0 - 1, COLS], F32R)
        wh0 = sb("wh0", [P, U0, N], F32R)
        wl0 = sb("wl0", [P, U0 - 1, N], F32R)
        wh1 = sb("wh1", [P, F * N], F32R)
        wl1 = sb("wl1", [P, F * N], F32R)
        yh = [sb(f"yh{p}", [P, COLS], F32R) for p in range(2)]
        yl = [sb(f"yl{p}", [P, COLS], F32R) for p in range(2)]
        parts = sb("parts", [P, DC, max(PARTS), N])
        pooled = sb("pooled", [P, 2, 2 * max(PAIR), N])
        paired_sum = sb("paired_sum", [P, max(PAIR), N])
        y1 = sb("y1", [P, DC, N])
        acc0 = sb("acc0", [P, COLS])
        acc1 = sb("acc1", [P, COLS])
        sum0 = sb("sum0", [P, P])
        sum1 = sb("sum1", [P, N])
        sum1_t = sb("sum1_t", [P, P])
        dense_t = sb("dense_t", [P, B])
        w1 = sb("w1", [P, 3, H1])
        w2 = sb("w2", [P, H1 // P, H2])
        w3 = sb("w3", [P, H2 // P])
        b1 = sb("b1", [P, H1 // P])
        b2 = sb("b2", [P, H2 // P])
        h1 = sb("h1", [P, H1 // P, P])
        h2 = sb("h2", [P, H2 // P, P])
        ident = sb("ident", [P, P])
        y_out = sb("y_out", [1, P])

        w1_raw = parts[:, 0:2, :, :].rearrange("p e u n -> p (e u n)")
        w0_raw = z[:, 0:2, :].rearrange("p a (j n) -> p (a j) n", n=N)
        w0_swap = z[:, 2:3, :].rearrange("p a (j n) -> p (a j) n", n=N)
        dense = z[:, 3, 0:P]
        dense_turn = z[:, 3, P:2 * P]

        ps_a = [ps(f"ps_a{p}", [P, COLS]) for p in range(A_RING)]
        ps_d = [ps(f"ps_d{p}", [P, COLS]) for p in range(D_RING)]
        ps_0 = ps("ps_0", [P, COLS])
        ps_x = ps_0
        ps_y = ps_x[0:1, H2:H2 + P]

        idx_loaded = sem("idx_loaded")
        gathered = sem("gathered")
        t_filled = sem("t_filled")
        t_copied = sem("t_copied")
        x_written = [sem(f"x_written{k}") for k in range(2)]
        x_loaded = [sem(f"x_loaded{p}") for p in range(2)]
        z_made = sem("z_made")
        zh_made = sem("zh_made")
        zl_made = sem("zl_made")
        unit_done = sem("unit_done")
        yh_made = sem("yh_made")
        yl_made = sem("yl_made")
        act_filled = sem("act_filled")
        dve_filled = sem("dve_filled")
        act_taken = sem("act_taken")
        dve_taken = sem("dve_taken")
        paired = sem("paired")
        folded = sem("folded")
        reduced = sem("reduced")
        acc0_made = sem("acc0_made")
        acc1_made = sem("acc1_made")
        sum0_made = sem("sum0_made")
        sum1_made = sem("sum1_made")
        sum1_turned = sem("sum1_turned")
        sum1_copied = sem("sum1_copied")
        ident_zero = sem("ident_zero")
        ident_made = sem("ident_made")
        w0_zeros = sem("w0_zeros")
        xs_zeros = sem("xs_zeros")
        pad_zeros = sem("pad_zeros")
        f0_doubled = sem("f0_doubled")
        w0_loaded = sem("w0_loaded")
        w1_loaded = [sem(f"w1_loaded{k}") for k in range(4)]
        mlp_loaded = sem("mlp_loaded")
        dense_loaded = sem("dense_loaded")
        dense_turned = sem("dense_turned")
        dense_copied = sem("dense_copied")
        dense_ready = sem("dense_ready")
        w0_summed = sem("w0_summed")
        wh0_made = sem("wh0_made")
        wh1_made = sem("wh1_made")
        w0_ready = sem("w0_ready")
        w1_ready = sem("w1_ready")
        h1_filled = sem("h1_filled")
        h1_made = sem("h1_made")
        h2_filled = sem("h2_filled")
        h2_made = sem("h2_made")
        y_filled = sem("y_filled")
        y_made = sem("y_made")
        out_written = sem("out_written")

        W1_PART = F * N // 4

        def w0_load(s):
            src = f0_m[0:1, 0, :]
            rows_hm = bass.AP(src.tensor, src.offset + s * N, [[(2 * F + 1) * N, F], [4 * N, 4], [1, N]])
            shift_16 = bass.AP(src.tensor, src.offset + F // 2 * N, [[(2 * F + 1) * N, F], [1, N]])
            src = f0_h[0:1, 0, :]
            j0 = 1 if s == 0 else 0
            rows_mh = bass.AP(src.tensor, src.offset + (4 * j0 + s) * F * N,
                              [[(F + 1) * N, F], [4 * F * N, 4 - j0], [1, N]])
            part = slice(32 * s, 32 * s + 32)
            loads = [(w0_raw[part, 0:4, :], rows_hm), (w0_swap[part, j0:4, :], rows_mh)]
            return loads + [(w0_raw[part, U0 - 1, :], shift_16)] * (s < 3)

        block = ctx.enter_context(nc.Block())

        @block.sync
        def _(sp):
            def load_idx(t):
                sp.dma_start(idx[:, :], ids[bass.ds(t * P, P), :]).then_inc(idx_loaded, NDMA)

            def load_x(t, q):
                p = q % 2
                src = x_dram[t, 0:1, q * COLS:(q + 1) * COLS]
                plain = bass.AP(src.tensor, src.offset, [[0, 4], [XROW, F], [1, COLS]])
                sp.dma_start(xp[p][:, 0, :], plain).then_inc(x_loaded[p], NDMA)
                for s in range(4):
                    part = slice(32 * s, 32 * s + 32)
                    shifted = bass.AP(src.tensor, src.offset + s * XROW, [[XROW, F], [4 * XROW, 4], [1, COLS]])
                    sp.dma_start(xs[p][part, 0:4, :], shifted).then_inc(x_loaded[p], NDMA)
                shift_16 = bass.AP(src.tensor, src.offset + F // 2 * XROW, [[0, 3], [XROW, F], [1, COLS]])
                sp.dma_start(xs[p][0:3 * F, U0 - 1, :], shift_16).then_inc(x_loaded[p], NDMA)

            load_idx(0)
            f0 = filter_0[0].rearrange("(h m) n -> h m n", m=F)
            for r in (0, F):
                sp.dma_start(f0_m[:, r:r + F, :], f0).then_inc(f0_doubled, NDMA)
                sp.dma_start(f0_h[r:r + F, :, :], f0).then_inc(f0_doubled, NDMA)
            sp.wait_ge(w0_zeros, 1)
            sp.wait_ge(f0_doubled, 4 * NDMA)
            for s in range(4):
                for dst, src in w0_load(s):
                    sp.dma_start(dst, src).then_inc(w0_loaded, NDMA)
            sp.wait_ge(xs_zeros, 1)

            def body(t, last):
                for q in range(QS):
                    if q < 2:
                        sp.wait_ge(x_written[q], 2 * NDMA * (t + 1))
                    if q == 1 and not last:
                        load_idx(t + 1)
                    if q and some(UNIT_N * (QS * t + q - 1)):
                        sp.wait_ge(z_made, UNIT_N * (QS * t + q - 1))
                    load_x(t, q)

            UNIT_N = len(UNITS)
            body(0, False)
            with sp.Fori(1, TILES - 1) as t:
                body(t, False)
            body(TILES - 1, True)
            sp.wait_ge(out_written, NDMA * TILES)

        @block.gpsimd
        def _(pool):
            def gather(f, par):
                nc.gpsimd.indirect_dma_start(
                    out=rows[par][:, f * D:(f + 1) * D], out_offset=None, in_=tables[f][:, :],
                    in_offset=bass.IndirectOffsetOnAxis(ap=idx[:, f:f + 1], axis=0)).then_inc(gathered, NDMA)

            def low_part(v, u):
                js = slice(UNITS[u][0], UNITS[u][-1] + 1)
                pool.wait_ge(zh_made, 3 * v + u + 1)
                if u == 2:
                    part = slice(0, F)
                    nc.gpsimd.tensor_tensor(zh[part, js, :], z[part, js, :], zh[part, js, :].bitcast(F32),
                                            ALU.subtract).then_inc(zl_made, 1)
                    return
                nc.gpsimd.tensor_tensor(zl[:, js, :], z[:, js, :], zh[:, js, :].bitcast(F32),
                                        ALU.subtract).then_inc(zl_made, 1)

            def pair(g, r):
                if some(g):
                    pool.wait_ge(folded, g)
                pool.wait_ge(act_taken, NA * g + POOLED[r])
                nc.gpsimd.tensor_tensor(paired_sum[:, 0:PAIR[r], :], pooled[:, r % 2, 0:PAIR[r], :],
                                        pooled[:, r % 2, PAIR[r]:2 * PAIR[r], :], ALU.add).then_inc(paired, 1)

            def fold(g, r):
                pool.wait_ge(paired, g + 1)
                if some(g - DC + 1):
                    pool.wait_ge(reduced, g - DC + 1)
                nc.gpsimd.tensor_tensor(parts[:, r, G_AT[r]:PARTS[r], :], paired_sum[:, 0:FOLD[r], :],
                                        paired_sum[:, FOLD[r]:PAIR[r], :], ALU.add).then_inc(folded, 1)

            nc.gpsimd.memset(ident[:, :], 0.0).then_inc(ident_zero, 1)
            pool.wait_ge(ident_zero, 1)
            nc.gpsimd.affine_select(out=ident[:, :], in_=ident[:, :], compare_op=ALU.not_equal, fill=1.0, base=0,
                                    pattern=[[-1, P]], channel_multiplier=1).then_inc(ident_made, 1)
            pool.wait_ge(idx_loaded, NDMA)
            for f in range(F):
                gather(f, 0)
            for u in range(3):
                low_part(0, u)

            def body(t, par, last):
                f = 0
                for q in range(QS):
                    c = QS * t + q
                    for what, r in POOL_STEPS:
                        if what == "pair":
                            if q == 0 and r == 0 and not last:
                                pool.wait_ge(idx_loaded, NDMA * (t + 2))
                                if some(QS * DC * NV * t):
                                    pool.wait_ge(dve_taken, QS * DC * NV * t)
                            pair(DC * c + r, r)
                        elif what == "fold":
                            fold(DC * c + r, r)
                        elif what == "low":
                            if not (last and q == QS - 1):
                                low_part(c + 1, r)
                        elif r < GATHERS[q] and not last:
                            gather(f, 1 - par)
                            f += 1

            body(0, 0, False)
            with pool.Fori(0, TILES // 2 - 1) as k:
                body(2 * k + 1, 1, False)
                body(2 * k + 2, 0, False)
            body(TILES - 1, 1, True)

        @block.scalar
        def _(act):
            def take_bank(t, q, e, a, par):
                g = DC * (QS * t + q) + e
                slot = (NA * (DC * q + e) + a) % A_RING
                if a == 0 and some(g - 1):
                    act.wait_ge(paired, g - 1)
                if a == POOLED[e] and some(g - DC + 1):
                    act.wait_ge(reduced, g - DC + 1)
                act.wait_ge(act_filled, NA * g + a + 1)
                for i in range(HB):
                    h = HB * A_BANKS[a] + i
                    to = (pooled[:, e % 2, HB * a + i, :] if a < POOLED[e]
                          else parts[:, e, A_AT + HB * (a - POOLED[e]) + i, :])
                    x = h * D + DC * q + e
                    ins = nc.scalar.activation(to, ps_a[slot][:, i * N:(i + 1) * N], ACT.Copy,
                                               scale=rows[par][:, x:x + 1])
                ins.then_inc(act_taken, 1)

            def high_part(v, u):
                js = slice(UNITS[u][0], UNITS[u][-1] + 1)
                act.wait_ge(z_made, 3 * v + u + 1)
                if some(3 * (v - 1) + u + 1):
                    act.wait_ge(unit_done, 3 * (v - 1) + u + 1)
                nc.scalar.activation(zh[:, js, :], z[:, js, :], ACT.Copy).then_inc(zh_made, 1)

            def high_y0(v, p):
                act.wait_ge(unit_done, 3 * (v + 1))
                nc.scalar.activation(yh[p][:, :], ps_0[:, :], ACT.Relu).then_inc(yh_made, 1)

            def copy_x(t, k):
                act.wait_ge(t_filled, 2 * t + k + 1)
                if some(t):
                    act.wait_ge(x_written[k], 2 * NDMA * t)
                nc.scalar.activation(xt[:, k, :], ps_x[:, :], ACT.Copy).then_inc(t_copied, 1)
                act.wait_ge(t_copied, 2 * t + k + 1)
                for r in (0, F):
                    act.dma_start(x_dram[t, r:r + F, :].rearrange("f (g a c) -> (f g) a c", g=4, a=2)[:, k, :],
                                  xt[:, k, :]).then_inc(x_written[k], NDMA)

            def copy_sum1(t):
                act.wait_ge(sum1_turned, t + 1)
                nc.scalar.activation(sum1_t[:, :], ps_x[:, 0:P], ACT.Copy).then_inc(sum1_copied, 1)

            def relu_h1(t):
                act.wait_ge(h1_filled, t + 1)
                for m in range(H1 // P):
                    ins = nc.scalar.activation(h1[:, m, :], ps_x[:, m * P:(m + 1) * P], ACT.Relu, bias=b1[:, m:m + 1])
                ins.then_inc(h1_made, 1)

            def relu_h2(t):
                act.wait_ge(h2_filled, t + 1)
                for m in range(H2 // P):
                    ins = nc.scalar.activation(h2[:, m, :], ps_x[:, m * P:(m + 1) * P], ACT.Relu, bias=b2[:, m:m + 1])
                ins.then_inc(h2_made, 1)

            def store_y(t):
                if some(t):
                    act.wait_ge(out_written, NDMA * t)
                act.wait_ge(y_filled, t + 1)
                nc.scalar.activation(y_out[:, :], ps_y, ACT.Copy).then_inc(y_made, 1)
                act.wait_ge(y_made, t + 1)
                act.dma_start(out[bass.ds(t * P, P), :].rearrange("b a -> a b"), y_out[:, :]).then_inc(out_written, NDMA)

            act.dma_start(dense.rearrange("p (k c) -> p k c", c=ND),
                          dense_ctx.rearrange("(k p) c -> p k c", p=P)).then_inc(dense_loaded, NDMA)
            for k in range(4):
                hs = slice(k * F // 4, (k + 1) * F // 4)
                act.dma_start(w1_raw[:, k * W1_PART:(k + 1) * W1_PART].rearrange("p (h n) -> p h n", n=N),
                              filter_1[0].rearrange("(h m) n -> m h n", m=N)[:, hs, :]).then_inc(w1_loaded[k], NDMA)
            act.dma_start(w1[:, 0:2, :], W_top1[0:2 * P, :].rearrange("(k p) n -> p k n", p=P)).then_inc(mlp_loaded, NDMA)
            act.dma_start(w2[:, :, :], W_top2.rearrange("(k p) n -> p k n", p=P)).then_inc(mlp_loaded, NDMA)
            act.dma_start(w3[:, :], W_top3.rearrange("(k p) a -> p (k a)", p=P),
                          allow_slow_non_contiguous=True).then_inc(mlp_loaded, NDMA)
            act.dma_start(b1[:, :], b_top1.rearrange("(k p) -> p k", p=P),
                          allow_slow_non_contiguous=True).then_inc(mlp_loaded, NDMA)
            act.dma_start(b2[:, :], b_top2.rearrange("(k p) -> p k", p=P),
                          allow_slow_non_contiguous=True).then_inc(mlp_loaded, NDMA)
            act.wait_ge(pad_zeros, 1)
            act.dma_start(w1[0:ND, 2, :], W_top1[2 * P:2 * P + ND, :]).then_inc(mlp_loaded, NDMA)

            act.wait_ge(dense_turned, 1)
            nc.scalar.activation(dense_turn, ps_x[:, 0:P], ACT.Copy).then_inc(dense_copied, 1)
            act.wait_ge(dense_copied, 1)
            for k in range(TILES):
                act.dma_start(dense_t[0:ND, k * P:(k + 1) * P], dense_turn[ND * k:ND * k + ND, :]).then_inc(
                    dense_ready, NDMA)
            act.wait_ge(w0_summed, 1)
            nc.scalar.activation(wh0[:, :, :], w0_raw[:, 0:U0, :], ACT.Copy).then_inc(wh0_made, 1)
            for k in range(4):
                cols = slice(k * W1_PART, (k + 1) * W1_PART)
                act.wait_ge(w1_loaded[k], NDMA)
                nc.scalar.activation(wh1[:, cols], w1_raw[:, cols], ACT.Copy).then_inc(wh1_made, 1)
            copy_x(0, 0)
            copy_x(0, 1)
            for u in range(3):
                high_part(0, u)
            high_y0(0, 0)

            def body(t, par, last):
                for q in range(QS):
                    c = QS * t + q
                    for e in range(DC):
                        for k in range(8):
                            if k in A_BANKS:
                                take_bank(t, q, e, A_BANKS.index(k), par)
                            if (e, k) in ZH_AT and not (last and q == QS - 1):
                                high_part(c + 1, ZH_AT.index((e, k)))
                            if (e, k) == YH_AT and not (last and q == QS - 1):
                                high_y0(c + 1, (q + 1) % 2)
                            if (q, e, k) in T_COPY and not last:
                                copy_x(t + 1, T_COPY.index((q, e, k)))
                            if some(t):
                                if (q, e, k) == TURN_COPY:
                                    copy_sum1(t - 1)
                                if (q, e, k) == H1_RELU:
                                    relu_h1(t - 1)
                                if (q, e, k) == H2_RELU:
                                    relu_h2(t - 1)
                                if (q, e, k) == Y_COPY:
                                    store_y(t - 1)

            body(0, 0, False)
            with act.Fori(0, TILES // 2 - 1) as k:
                body(2 * k + 1, 1, False)
                body(2 * k + 2, 0, False)
            body(TILES - 1, 1, True)
            copy_sum1(TILES - 1)
            relu_h1(TILES - 1)
            relu_h2(TILES - 1)
            store_y(TILES - 1)

        @block.vector
        def _(dve):
            def take_bank(t, q, e, a, par):
                g = DC * (QS * t + q) + e
                slot = (NV * (DC * q + e) + a) % D_RING
                if a == 0 and some(g - DC + 1):
                    dve.wait_ge(reduced, g - DC + 1)
                dve.wait_ge(dve_filled, NV * g + a + 1)
                h, d = HB * D_BANKS[a], DC * q + e
                x = rows[par][:, :].rearrange("p (f d) -> p f d", d=D)[:, h:h + HB, d:d + 1]
                nc.vector.tensor_tensor(parts[:, e, HB * a:HB * (a + 1), :],
                                        ps_d[slot][:, :].rearrange("p (h n) -> p h n", n=N),
                                        x.broadcast_to((P, HB, N)), ALU.mult).then_inc(dve_taken, 1)

            def reduce_h(g, e, c):
                if e == 0 and some(c):
                    dve.wait_ge(acc1_made, c)
                dve.wait_ge(dve_taken, NV * (g + 1))
                dve.wait_ge(act_taken, NA * (g + 1))
                dve.wait_ge(folded, g + 1)
                nc.vector.tensor_reduce(y1[:, e, :], parts[:, e, 0:PARTS[e], :].rearrange("p u n -> p n u"), AX.X,
                                        ALU.add).then_inc(reduced, 1)

            def add_1(c, starts):
                dve.wait_ge(reduced, DC * (c + 1))
                y = y1[:, :, :].rearrange("p e n -> p (e n)")
                if starts:
                    nc.vector.tensor_scalar(acc1[:, :], y, 0.0, None, ALU.max).then_inc(acc1_made, 1)
                else:
                    nc.vector.scalar_tensor_tensor(out=acc1[:, :], in0=y, scalar=0.0, in1=acc1[:, :],
                                                   op0=ALU.max, op1=ALU.add).then_inc(acc1_made, 1)

            def product(t, q, u):
                v, p = QS * t + q, q % 2
                js = slice(UNITS[u][0], UNITS[u][-1] + 1)
                if u == 0:
                    dve.wait_ge(x_loaded[p], X_LOADS * NDMA * (QS // 2 * t + q // 2 + 1))
                if some(3 * (v - 1) + u + 1):
                    dve.wait_ge(zl_made, 3 * (v - 1) + u + 1)
                nc.vector.tensor_tensor(z[:, js, :], xs[p][:, js, :],
                                        xp[p][:, :, :].broadcast_to((P, len(UNITS[u]), COLS)),
                                        ALU.mult).then_inc(z_made, 1)

            def low_y0(v, p):
                dve.wait_ge(yh_made, v + 1)
                nc.vector.scalar_tensor_tensor(out=yl[p][:, :], in0=ps_0[:, :], scalar=0.0,
                                               in1=yh[p][:, :].bitcast(F32), op0=ALU.max,
                                               op1=ALU.subtract).then_inc(yl_made, 1)

            def add_0(v, starts):
                if starts:
                    nc.vector.tensor_scalar(acc0[:, :], ps_0[:, :], 0.0, None, ALU.max).then_inc(acc0_made, 1)
                else:
                    dve.wait_ge(acc0_made, v)
                    nc.vector.scalar_tensor_tensor(out=acc0[:, :], in0=ps_0[:, :], scalar=0.0, in1=acc0[:, :],
                                                   op0=ALU.max, op1=ALU.add).then_inc(acc0_made, 1)

            def finish_sum(t, acc, acc_made, total, total_made):
                dve.wait_ge(acc_made, QS * (t + 1))
                if some(t):
                    dve.wait_ge(h1_filled, t)
                nc.vector.tensor_reduce(total[:, :], acc[:, :].rearrange("p (e b) -> p b e", b=P), AX.X,
                                        ALU.add).then_inc(total_made, 1)

            nc.vector.memset(w0_raw[:, U0 - 1, :], 0.0)
            nc.vector.memset(w0_swap[:, 0, :], 0.0).then_inc(w0_zeros, 1)
            nc.vector.memset(w1[:, 2, :], 0.0)
            nc.vector.memset(dense_t[:, :], 0.0).then_inc(pad_zeros, 1)
            nc.vector.memset(xs[0][:, U0 - 1, :], 0.0)
            nc.vector.memset(xs[1][:, U0 - 1, :], 0.0).then_inc(xs_zeros, 1)
            dve.wait_ge(w0_loaded, 11 * NDMA)
            nc.vector.tensor_tensor(w0_raw[:, 0:4, :], w0_raw[:, 0:4, :], w0_swap[:, 0:4, :],
                                    ALU.add).then_inc(w0_summed, 1)
            dve.wait_ge(wh0_made, 1)
            nc.vector.tensor_tensor(wl0[:, :, :], w0_raw[:, 0:4, :], wh0[:, 0:4, :].bitcast(F32),
                                    ALU.subtract)
            part = slice(2 * F, 3 * F)
            nc.vector.tensor_tensor(wh0[part, U0 - 1, :], w0_raw[part, U0 - 1, :],
                                    wh0[part, U0 - 1, :].bitcast(F32), ALU.subtract).then_inc(w0_ready, 1)
            for k in range(4):
                cols = slice(k * W1_PART, (k + 1) * W1_PART)
                dve.wait_ge(wh1_made, k + 1)
                nc.vector.tensor_tensor(wl1[:, cols], w1_raw[:, cols], wh1[:, cols].bitcast(F32),
                                        ALU.subtract).then_inc(w1_ready, 1)
            dve.wait_ge(dense_ready, TILES * NDMA)
            dve.wait_ge(w0_ready, 1)
            for u in range(3):
                product(0, 0, u)
            low_y0(0, 0)
            add_0(0, True)

            def body(t, par, last):
                for q in range(QS):
                    c = QS * t + q
                    more = not (last and q == QS - 1)
                    for e in range(DC):
                        for k in range(8):
                            if k in D_BANKS:
                                take_bank(t, q, e, D_BANKS.index(k), par)
                            if (e, k) in Z_AT and more:
                                product(t, q + 1, Z_AT.index((e, k)))
                            if k == REDUCE_K and some(DC * c + e):
                                reduce_h(DC * c + e - 1, (e - 1) % DC, c)
                            if (e, k) == RELU_AT and some(c):
                                add_1(c - 1, q == 1)
                            if (q, e, k) == SUM1_AT and some(t):
                                finish_sum(t - 1, acc1, acc1_made, sum1, sum1_made)
                            if (q, e, k) == SUM0_AT:
                                finish_sum(t, acc0, acc0_made, sum0, sum0_made)
                            if (e, k) == YL_AT and more:
                                low_y0(c + 1, (q + 1) % 2)
                            if (e, k) == ACC0_AT and more:
                                add_0(c + 1, q == QS - 1)

            body(0, 0, False)
            with dve.Fori(0, TILES // 2 - 1) as k:
                body(2 * k + 1, 1, False)
                body(2 * k + 2, 0, False)
            body(TILES - 1, 1, True)
            reduce_h(D * TILES - 1, DC - 1, NCH - 1)
            add_1(NCH - 1, False)
            finish_sum(TILES - 1, acc1, acc1_made, sum1, sum1_made)

        @block.tensor
        def _(pe):
            def transpose_x(t, par, k):
                if k == 0:
                    pe.wait_ge(gathered, NDMA * F * (t + 1))
                    if some(QS * t - 1):
                        pe.wait_ge(acc0_made, QS * t - 1)
                else:
                    pe.wait_ge(t_copied, 2 * t + 1)
                for e in range(4):
                    ins = nc.tensor.matmul(ps_x[:, e * P:(e + 1) * P], rows[par][:, 4 * k + e:F * D:8],
                                           ident[:, :], start=True, stop=True, is_transpose=True)
                ins.then_inc(t_filled, 1)

            def unit(v, u, between=None):
                if u == 0 and some(v):
                    pe.wait_ge(acc0_made, v)
                if u == 0 and between:
                    pe.wait_ge(*between)
                js = UNITS[u]
                if u == 2:
                    pe.wait_ge(zl_made, 3 * v + u + 1)
                    nc.tensor.matmul(ps_0[:, :], wh0[:, U0 - 1, :], zh[:, U0 - 1, :], start=False,
                                     stop=True).then_inc(unit_done, 1)
                    return
                pe.wait_ge(zh_made, 3 * v + u + 1)
                for j in js:
                    nc.tensor.matmul(ps_0[:, :], wh0[:, j, :], zh[:, j, :], start=j == 0, stop=False)
                    nc.tensor.matmul(ps_0[:, :], wl0[:, j, :], zh[:, j, :], start=False, stop=False)
                pe.wait_ge(zl_made, 3 * v + u + 1)
                for j in js:
                    ins = nc.tensor.matmul(ps_0[:, :], wh0[:, j, :], zl[:, j, :], start=False, stop=False)
                ins.then_inc(unit_done, 1)

            def bank(t, q, e, k):
                g = DC * (QS * t + q) + e
                if k in A_BANKS:
                    n, at, filled, taken = NA, ps_a, act_filled, act_taken
                    a, ring = A_BANKS.index(k), A_RING
                else:
                    n, at, filled, taken = NV, ps_d, dve_filled, dve_taken
                    a, ring = D_BANKS.index(k), D_RING
                to = at[(n * (DC * q + e) + a) % ring]
                if some(n * g + a + 1 - ring):
                    pe.wait_ge(taken, n * g + a + 1 - ring)
                high = yh[q % 2][:, e * P:(e + 1) * P]
                low = yl[q % 2][:, e * P:(e + 1) * P]
                cols = slice(k * COLS, (k + 1) * COLS)
                passes = [(low, wh1), (high, wh1), (high, wl1)]
                if k % 2:
                    passes.reverse()
                for i, (y, w) in enumerate(passes):
                    ins = nc.tensor.matmul(to[:, :], y, w[:, cols], start=i == 0, stop=i == 2)
                ins.then_inc(filled, 1)

            def turn_sum1(t, last):
                pe.wait_ge(sum1_made, t + 1)
                pe.wait_ge(acc0_made, QS * (t + 1) if last else QS * (t + 1) + 2)
                nc.tensor.matmul(ps_x[:, 0:P], sum1[:, :], ident[:, :], start=True, stop=True,
                                 is_transpose=True).then_inc(sum1_turned, 1)

            def perceptron_1(t):
                pe.wait_ge(sum0_made, t + 1)
                pe.wait_ge(sum1_copied, t + 1)
                for m in range(H1 // P):
                    for k, x in ((0, sum0[:, :]), (1, sum1_t[:, :]), (2, dense_t[:, bass.ds(t * P, P)])):
                        ins = nc.tensor.matmul(ps_x[:, m * P:(m + 1) * P], w1[:, k, m * P:(m + 1) * P], x,
                                               start=k == 0, stop=k == 2)
                ins.then_inc(h1_filled, 1)

            def perceptron_2(t, last=False):
                pe.wait_ge(h1_made, t + 1)
                if not last:
                    pe.wait_ge(acc0_made, QS * (t + 1) + 3)
                for m in range(H2 // P):
                    for k in range(H1 // P):
                        ins = nc.tensor.matmul(ps_x[:, m * P:(m + 1) * P], w2[:, k, m * P:(m + 1) * P], h1[:, k, :],
                                               start=k == 0, stop=k == H1 // P - 1)
                ins.then_inc(h2_filled, 1)

            def perceptron_3(t):
                pe.wait_ge(h2_made, t + 1)
                for k in range(H2 // P):
                    ins = nc.tensor.matmul(ps_y, w3[:, k:k + 1], h2[:, k, :], start=k == 0, stop=k == H2 // P - 1)
                ins.then_inc(y_filled, 1)

            pe.wait_ge(ident_made, 1)
            pe.wait_ge(dense_loaded, NDMA)
            nc.tensor.matmul(ps_x[:, 0:P], dense, ident[:, :], start=True, stop=True,
                             is_transpose=True).then_inc(dense_turned, 1)
            pe.wait_ge(dense_copied, 1)
            transpose_x(0, 0, 0)
            transpose_x(0, 0, 1)
            pe.wait_ge(w0_ready, 1)
            for u in range(3):
                unit(0, u, (t_copied, 2))
            pe.wait_ge(w1_ready, 4)

            def body(t, par, last):
                for q in range(QS):
                    c = QS * t + q
                    pe.wait_ge(yl_made, c + 1)
                    between = None
                    if q == T_MM[1][0] and not last:
                        between = (t_copied, 2 * (t + 2))
                    if q == H1_RELU[0] and some(t):
                        between = (h1_made, t)
                    if q == Y_COPY[0] and some(t):
                        between = (y_made, t)
                    for e in range(DC):
                        for k in range(8):
                            bank(t, q, e, k)
                            if (e, k) in MM_AT and not (last and q == QS - 1):
                                unit(c + 1, MM_AT.index((e, k)), between)
                            if (q, e, k) in T_MM and not last:
                                transpose_x(t + 1, 1 - par, T_MM.index((q, e, k)))
                            if some(t):
                                if (q, e, k) == TURN_MM:
                                    turn_sum1(t - 1, False)
                                if (q, e, k) == H1_MM:
                                    perceptron_1(t - 1)
                                if (q, e, k) == H2_MM:
                                    perceptron_2(t - 1)
                                if (q, e, k) == Y_MM:
                                    perceptron_3(t - 1)

            body(0, 0, False)
            pe.wait_ge(mlp_loaded, 6 * NDMA)
            pe.wait_ge(dense_ready, TILES * NDMA)
            with pe.Fori(0, TILES // 2 - 1) as k:
                body(2 * k + 1, 1, False)
                body(2 * k + 2, 0, False)
            body(TILES - 1, 1, True)
            turn_sum1(TILES - 1, True)
            perceptron_1(TILES - 1)
            perceptron_2(TILES - 1, True)
            perceptron_3(TILES - 1)


_TABLES = [f"tbl_{f}" for f in range(F)]
_INS = (["dense_ctx", "ids"] + _TABLES
        + ["W_top1", "b_top1", "W_top2", "b_top2", "W_top3", "L0_rec_filter_0", "L0_rec_filter_1"])


def kernel(**inputs):
    import numpy as np
    from concourse import bacc
    from concourse.bass_utils import run_bass_kernel_spmd

    nc = bacc.Bacc("TRN2", target_bir_lowering=False, num_devices=1)
    arrays, aps = {}, {}
    for name in _INS:
        a = np.ascontiguousarray(inputs[name])
        arrays[f"in_{name}"] = a
        aps[name] = nc.dram_tensor(f"in_{name}", a.shape, mybir.dt.from_np(a.dtype), kind="ExternalInput").ap()
    out = nc.dram_tensor("out_y", (B, 1), F32, kind="ExternalOutput").ap()
    build(nc, aps["dense_ctx"], aps["ids"], [aps[k] for k in _TABLES], aps["W_top1"], aps["b_top1"],
          aps["W_top2"], aps["b_top2"], aps["W_top3"], aps["L0_rec_filter_0"], aps["L0_rec_filter_1"], out)
    r = run_bass_kernel_spmd(nc, [arrays], core_ids=[0])
    return r.results[0]["out_y"]
```
